# Optimizing a Trainium2 kernel written in Bass

```python
import numpy as np
import jax
import jax.numpy as jnp

def _softmax(x, axis=-1):
    return jax.nn.softmax(x, axis=axis)

def _gelu(x):
    return jax.nn.gelu(x, approximate=True)

def _silu(x):
    return jax.nn.silu(x)

def _sigmoid(x):
    return jax.nn.sigmoid(x)

def _layernorm(x, axis=-1, eps=1e-05):
    m = jnp.mean(x, axis=axis, keepdims=True)
    v = jnp.var(x, axis=axis, keepdims=True)
    return (x - m) / jnp.sqrt(v + eps)

def _scatter_add(tgt, idx, src, axis=0):
    return tgt.at[idx].add(src)

def _segment_sum(src, seg, n):
    return jax.ops.segment_sum(src, seg, n)
kernel_name = 'mk_macaron_d1_jaxref_r8_2db1e5'

def setup_inputs(seed: int=0):
    np.random.seed(seed)
    _w = jnp.asarray

    def _L0_attn_setup():
        import jax, jax.numpy as jnp
        import numpy as np
        DIM = 128
        B, T = (4, 1024)
        key = jax.random.key(seed)
        ks = jax.random.split(key, 5)
        scale = 1.0 / np.sqrt(DIM)
        x = jax.random.normal(ks[0], (B, T, DIM), dtype=jnp.float32)
        w_in = jax.random.uniform(ks[1], (DIM, DIM), jnp.float32, -scale, scale)
        b_in = jax.random.uniform(ks[2], (DIM,), jnp.float32, -scale, scale)
        a = jnp.zeros((DIM,), jnp.float32)
        b = jnp.ones((DIM,), jnp.float32)
        w_out = jax.random.uniform(ks[3], (DIM, DIM), jnp.float32, -scale, scale)
        b_out = jax.random.uniform(ks[4], (DIM,), jnp.float32, -scale, scale)
        return {'x': x, 'w_in': w_in, 'b_in': b_in, 'a': a, 'b': b, 'w_out': w_out, 'b_out': b_out}
    _L0_attn_in = _L0_attn_setup()

    def _L0_ffn_setup():
        import jax, jax.numpy as jnp
        import numpy as np
        DIM = 128
        DEPTH = 6
        HEADS = 16
        DIM_HEAD = 64
        WINDOW = 32
        INNER = HEADS * DIM_HEAD
        DIM_INNER = int(DIM * 4 * 2 / 3)
        QK_SCALE = 8.0

        def shift_tokens(t):
            a, s = jnp.split(t, 2, -1)
            s = jnp.pad(s, ((0, 0), (1, 0), (0, 0)))[:, :-1]
            return jnp.concatenate([a, s], -1)

        def l2norm(t):
            return t / jnp.maximum(jnp.linalg.norm(t, axis=-1, keepdims=True), 1e-12)

        def rotate_half(x):
            x1, x2 = jnp.split(x, 2, -1)
            return jnp.concatenate([-x2, x1], -1)

        def rotary_tables(n):
            half = jnp.arange(0, DIM_HEAD, 2, dtype=jnp.float32)
            inv_freq = 1.0 / 10000.0 ** (half / DIM_HEAD)
            t = jnp.arange(n, dtype=jnp.float32)
            freqs = t[:, None] * inv_freq[None, :]
            freqs = jnp.concatenate([freqs, freqs], -1)
            base_scale = (half + 0.4 * DIM_HEAD) / (1.4 * DIM_HEAD)
            power = (t - n // 2) / (WINDOW // 2)
            scale = base_scale[None, :] ** power[:, None]
            scale = jnp.concatenate([scale, scale], -1)
            return (freqs, scale)

        def local_attention(q, k, v):
            b, h, n, d = q.shape
            w = WINDOW
            nw = n // w
            bq = q.reshape(b, h, nw, w, d)
            bk = k.reshape(b, h, nw, w, d)
            bv = v.reshape(b, h, nw, w, d)

            def look(t):
                p = jnp.pad(t, ((0, 0), (0, 0), (1, 0), (0, 0), (0, 0)))
                return jnp.concatenate([p[:, :, :nw], p[:, :, 1:]], axis=3)
            bk2, bv2 = (look(bk), look(bv))
            seq = jnp.arange(n).reshape(nw, w)
            seq_p = jnp.pad(seq, ((1, 0), (0, 0)), constant_values=-1)
            jt = jnp.concatenate([seq_p[:nw], seq_p[1:]], axis=1)
            it = seq[:, :, None]
            jb = jt[:, None, :]
            mask = (it < jb) | (it > jb + w) | (jb == -1)
            sim = jnp.einsum('bhwie,bhwje->bhwij', bq, bk2) * QK_SCALE
            sim = jnp.where(mask, -jnp.finfo(sim.dtype).max, sim)
            attn = jax.nn.softmax(sim, -1)
            out = jnp.einsum('bhwij,bhwje->bhwie', attn, bv2)
            return out.reshape(b, h, n, d)

        def attn_layer(x, Wqkv, qs, ksc, Wo):
            b, n, _ = x.shape
            qkv = x @ Wqkv
            q, k, v = jnp.split(qkv, 3, -1)
            sh = lambda t: t.reshape(b, n, HEADS, DIM_HEAD).transpose(0, 2, 1, 3)
            q, k, v = (sh(q), sh(k), sh(v))
            q = l2norm(q) * qs
            k = l2norm(k) * ksc
            freqs, scale = rotary_tables(n)
            cos, sin = (jnp.cos(freqs), jnp.sin(freqs))
            q = q * cos * scale + rotate_half(q) * sin * scale
            inv = 1.0 / scale
            k = k * cos * inv + rotate_half(k) * sin * inv
            out = local_attention(q, k, v)
            out = out.transpose(0, 2, 1, 3).reshape(b, n, INNER)
            return out @ Wo

        def ffn_layer(x, g, bln, W1, b1, W2, b2):
            mu = x.mean(-1, keepdims=True)
            var = ((x - mu) ** 2).mean(-1, keepdims=True)
            xn = (x - mu) / jnp.sqrt(var + 1e-05) * g + bln
            hg = xn @ W1 + b1
            a, gate = jnp.split(hg, 2, -1)
            return a * jax.nn.gelu(gate, approximate=False) @ W2 + b2
        key = jax.random.key(seed)
        ks = jax.random.split(key, 8)
        B, N = (2, 256)
        init = lambda k, shape: jax.random.normal(k, shape, jnp.float32) * 0.02
        return {'x': jax.random.normal(ks[0], (B, N, DIM), jnp.float32), 'Wqkv': init(ks[1], (DEPTH, DIM, 3 * INNER)), 'q_scale': jnp.ones((DEPTH, DIM_HEAD), jnp.float32), 'k_scale': jnp.ones((DEPTH, DIM_HEAD), jnp.float32), 'Wo': init(ks[2], (DEPTH, INNER, DIM)), 'ln_g': jnp.ones((DEPTH, DIM), jnp.float32), 'ln_b': jnp.zeros((DEPTH, DIM), jnp.float32), 'W1': init(ks[3], (DEPTH, DIM, 2 * DIM_INNER)), 'b1': jnp.zeros((DEPTH, 2 * DIM_INNER), jnp.float32), 'W2': init(ks[4], (DEPTH, DIM_INNER, DIM)), 'b2': jnp.zeros((DEPTH, DIM), jnp.float32)}
    _L0_ffn_in = _L0_ffn_setup()
    _d = {'L0_attn_x': _L0_attn_in['x'], 'L0_attn_w_in': _L0_attn_in['w_in'], 'L0_attn_b_in': _L0_attn_in['b_in'], 'L0_attn_a': _L0_attn_in['a'], 'L0_attn_b': _L0_attn_in['b'], 'L0_attn_w_out': _L0_attn_in['w_out'], 'L0_attn_b_out': _L0_attn_in['b_out'], 'L0_ffn_Wqkv': _L0_ffn_in['Wqkv'], 'L0_ffn_q_scale': _L0_ffn_in['q_scale'], 'L0_ffn_k_scale': _L0_ffn_in['k_scale'], 'L0_ffn_Wo': _L0_ffn_in['Wo'], 'L0_ffn_ln_g': _L0_ffn_in['ln_g'], 'L0_ffn_ln_b': _L0_ffn_in['ln_b'], 'L0_ffn_W1': _L0_ffn_in['W1'], 'L0_ffn_b1': _L0_ffn_in['b1'], 'L0_ffn_W2': _L0_ffn_in['W2'], 'L0_ffn_b2': _L0_ffn_in['b2']}
    _x0 = _d['L0_attn_x']
    _d['L0_attn_x'] = jax.random.normal(jax.random.fold_in(jax.random.key(seed), 1), (2, 1024, 128), dtype=_x0.dtype)
    del _x0
    return _d

def reference(L0_attn_x, L0_attn_w_in, L0_attn_b_in, L0_attn_a, L0_attn_b, L0_attn_w_out, L0_attn_b_out, L0_ffn_Wqkv, L0_ffn_q_scale, L0_ffn_k_scale, L0_ffn_Wo, L0_ffn_ln_g, L0_ffn_ln_b, L0_ffn_W1, L0_ffn_b1, L0_ffn_W2, L0_ffn_b2):

    def _L0_attn_ref(x, w_in, b_in, a, b, w_out, b_out):
        import jax, jax.numpy as jnp
        import numpy as np
        DIM = 128
        B, T = (4, 1024)
        h = jnp.einsum('btd,ed->bte', x, w_in) + b_in
        A = jax.nn.sigmoid(a)

        def step(state, h_t):
            state = A * state + b * h_t
            return (state, state)
        init = jnp.zeros_like(h[:, 0])
        _, ys = jax.lax.scan(step, init, jnp.swapaxes(h, 0, 1))
        y = jnp.swapaxes(ys, 0, 1)
        return jnp.einsum('btd,ed->bte', y, w_out) + b_out

    def _L0_ffn_ref(x, Wqkv, q_scale, k_scale, Wo, ln_g, ln_b, W1, b1, W2, b2):
        import jax, jax.numpy as jnp
        import numpy as np
        DIM = 128
        DEPTH = 6
        HEADS = 16
        DIM_HEAD = 64
        WINDOW = 32
        INNER = HEADS * DIM_HEAD
        DIM_INNER = int(DIM * 4 * 2 / 3)
        QK_SCALE = 8.0

        def shift_tokens(t):
            a, s = jnp.split(t, 2, -1)
            s = jnp.pad(s, ((0, 0), (1, 0), (0, 0)))[:, :-1]
            return jnp.concatenate([a, s], -1)

        def l2norm(t):
            return t / jnp.maximum(jnp.linalg.norm(t, axis=-1, keepdims=True), 1e-12)

        def rotate_half(x):
            x1, x2 = jnp.split(x, 2, -1)
            return jnp.concatenate([-x2, x1], -1)

        def rotary_tables(n):
            half = jnp.arange(0, DIM_HEAD, 2, dtype=jnp.float32)
            inv_freq = 1.0 / 10000.0 ** (half / DIM_HEAD)
            t = jnp.arange(n, dtype=jnp.float32)
            freqs = t[:, None] * inv_freq[None, :]
            freqs = jnp.concatenate([freqs, freqs], -1)
            base_scale = (half + 0.4 * DIM_HEAD) / (1.4 * DIM_HEAD)
            power = (t - n // 2) / (WINDOW // 2)
            scale = base_scale[None, :] ** power[:, None]
            scale = jnp.concatenate([scale, scale], -1)
            return (freqs, scale)

        def local_attention(q, k, v):
            b, h, n, d = q.shape
            w = WINDOW
            nw = n // w
            bq = q.reshape(b, h, nw, w, d)
            bk = k.reshape(b, h, nw, w, d)
            bv = v.reshape(b, h, nw, w, d)

            def look(t):
                p = jnp.pad(t, ((0, 0), (0, 0), (1, 0), (0, 0), (0, 0)))
                return jnp.concatenate([p[:, :, :nw], p[:, :, 1:]], axis=3)
            bk2, bv2 = (look(bk), look(bv))
            seq = jnp.arange(n).reshape(nw, w)
            seq_p = jnp.pad(seq, ((1, 0), (0, 0)), constant_values=-1)
            jt = jnp.concatenate([seq_p[:nw], seq_p[1:]], axis=1)
            it = seq[:, :, None]
            jb = jt[:, None, :]
            mask = (it < jb) | (it > jb + w) | (jb == -1)
            sim = jnp.einsum('bhwie,bhwje->bhwij', bq, bk2) * QK_SCALE
            sim = jnp.where(mask, -jnp.finfo(sim.dtype).max, sim)
            attn = jax.nn.softmax(sim, -1)
            out = jnp.einsum('bhwij,bhwje->bhwie', attn, bv2)
            return out.reshape(b, h, n, d)

        def attn_layer(x, Wqkv, qs, ksc, Wo):
            b, n, _ = x.shape
            qkv = x @ Wqkv
            q, k, v = jnp.split(qkv, 3, -1)
            sh = lambda t: t.reshape(b, n, HEADS, DIM_HEAD).transpose(0, 2, 1, 3)
            q, k, v = (sh(q), sh(k), sh(v))
            q = l2norm(q) * qs
            k = l2norm(k) * ksc
            freqs, scale = rotary_tables(n)
            cos, sin = (jnp.cos(freqs), jnp.sin(freqs))
            q = q * cos * scale + rotate_half(q) * sin * scale
            inv = 1.0 / scale
            k = k * cos * inv + rotate_half(k) * sin * inv
            out = local_attention(q, k, v)
            out = out.transpose(0, 2, 1, 3).reshape(b, n, INNER)
            return out @ Wo

        def ffn_layer(x, g, bln, W1, b1, W2, b2):
            mu = x.mean(-1, keepdims=True)
            var = ((x - mu) ** 2).mean(-1, keepdims=True)
            xn = (x - mu) / jnp.sqrt(var + 1e-05) * g + bln
            hg = xn @ W1 + b1
            a, gate = jnp.split(hg, 2, -1)
            return a * jax.nn.gelu(gate, approximate=False) @ W2 + b2
        for i in range(DEPTH):
            x = attn_layer(shift_tokens(x), Wqkv[i], q_scale[i], k_scale[i], Wo[i]) + x
            x = ffn_layer(shift_tokens(x), ln_g[i], ln_b[i], W1[i], b1[i], W2[i], b2[i]) + x
        return x
    x = L0_attn_x
    x = x + 0.5 * _L0_ffn_ref(_layernorm(x, axis=-1), L0_ffn_Wqkv, L0_ffn_q_scale, L0_ffn_k_scale, L0_ffn_Wo, L0_ffn_ln_g, L0_ffn_ln_b, L0_ffn_W1, L0_ffn_b1, L0_ffn_W2, L0_ffn_b2)
    x = x + _L0_attn_ref(_layernorm(x, axis=-1), L0_attn_w_in, L0_attn_b_in, L0_attn_a, L0_attn_b, L0_attn_w_out, L0_attn_b_out)
    x = x + 0.5 * _L0_ffn_ref(_layernorm(x, axis=-1), L0_ffn_Wqkv, L0_ffn_q_scale, L0_ffn_k_scale, L0_ffn_Wo, L0_ffn_ln_g, L0_ffn_ln_b, L0_ffn_W1, L0_ffn_b1, L0_ffn_W2, L0_ffn_b2)
    return x

_drawn_inputs = setup_inputs


def setup_inputs(seed=0):
    import zlib

    import numpy as np

    out = dict(_drawn_inputs(seed))
    spreads = {'L0_attn_a': (0.0, 0.8),
     'L0_attn_b': (1.0, 0.2),
     'L0_ffn_q_scale': (1.0, 0.6),
     'L0_ffn_k_scale': (1.0, 0.6),
     'L0_ffn_ln_g': (1.0, 0.6),
     'L0_ffn_ln_b': (0.0, 0.8),
     'L0_ffn_b1': (0.0, 0.8),
     'L0_ffn_b2': (0.0, 0.1)}
    factors = {'L0_ffn_W1': 3.268, 'L0_ffn_W2': 3.198, 'L0_attn_b_in': 2.7, 'L0_attn_b_out': 3.378}
    for name, (base, spread) in spreads.items():
        noise = np.random.default_rng([zlib.crc32(name.encode()), seed]).standard_normal(out[name].shape)
        drawn = base * np.exp(spread * noise) if base else spread * noise
        out[name] = jnp.asarray(drawn.astype(out[name].dtype))
    for name, factor in factors.items():
        out[name] = (out[name] * factor).astype(out[name].dtype)
    return out
```

```python
from contextlib import ExitStack

import numpy as np

import concourse.bass as bass
from concourse import mybir

F32 = mybir.dt.float32
BF16 = mybir.dt.bfloat16
I32 = mybir.dt.int32
ALU = mybir.AluOpType
ACT = mybir.ActivationFunctionType
AX = mybir.AxisListType.X

P = 128
DEPTH, HEADS, DH, WIN = 6, 16, 64, 32
BATCH, SEQ = 2, 1024
INNER = HEADS * DH
PAIRS = HEADS // 2
POS = SEQ // P
TILES = BATCH * POS
N = DEPTH * TILES
SLOTS = BATCH * (POS + 1)
FH = P * 4 * 2 // 3
FC = (FH + 2) // 3
QK_SCALE = 8.0
NEG = -1.0e30
NORM_EPS2 = 1e-24

L_X, L_QKV, L_ROT, L_S, L_AV, L_F, L_F2 = 0, 1, 2, 3, 4, 5, 6
FRONT = 6
UNROLL = 2


def macaron(nc, x_in, w_in, b_in, a_in, b_gain, w_out, b_out, w_qkv, q_scale, k_scale, w_o,
            ln_g, ln_b, w_1, b_1, w_2, b_2, c_rope, c_mask, c_ident, x2_dram, out):
    with ExitStack() as ctx:
        def sb(name, shape, dt=F32):
            return ctx.enter_context(nc.sbuf_tensor(name, [P] + shape, dt))

        def sem(name):
            return ctx.enter_context(nc.semaphore(name))

        Z = sb("Z", [SLOTS * P])
        qk = sb("qk", [2 * INNER])
        rot = sb("rot", [2 * INNER])
        swp = sb("swp", [INNER])
        sq = sb("sq", [INNER])
        kT = sb("kT", [PAIRS, WIN + 2 * P])
        qTz = sb("qTz", [PAIRS, 4, 2, WIN])
        prob = sb("prob", [PAIRS, 2, 2 * WIN])
        pTz = sb("pTz", [PAIRS, 4, 2, WIN])
        o_sb = sb("o_sb", [INNER])
        oT = sb("oT", [PAIRS, P])
        va = sb("va", [2, INNER])
        vb = sb("vb", [INNER])
        wq = sb("wq", [2, 3 * INNER])
        wo = sb("wo", [2 * PAIRS * P])
        tab = sb("tab", [2 * 4 * POS * DH])
        rope = sb("rope", [4 * POS * DH])
        scl = sb("scl", [DEPTH + 1, 4, DH])
        w1 = sb("w1", [DEPTH * 2 * FH])
        w2 = sb("w2", [DEPTH * 3 * P])
        bp = sb("bp", [DEPTH * 2 * FH])
        b2 = sb("b2", [DEPTH * P])
        mask = sb("mask", [2 * 512], BF16)
        idf = sb("idf", [P])
        idb = sb("idb", [P], BF16)
        idp = sb("idp", [P])
        xs = sb("xs", [2, P])
        xsT = sb("xsT", [2, P])
        xvT = sb("xvT", [2, P])
        xs2 = sb("xs2", [P])
        xn = sb("xn", [P])
        xnT = sb("xnT", [P])
        fa = sb("fa", [FH])
        fg = sb("fg", [FH])
        hh = sb("hh", [3 * FC])
        hT = sb("hT", [3, P])
        z2t = sb("z2t", [P])
        ssq = sb("ssq", [2 * HEADS])
        rn = sb("rn", [2 * HEADS])
        rt = sb("rt", [2 * HEADS])
        mx = sb("mx", [HEADS])
        rs = sb("rs", [HEADS])
        rr = sb("rr", [HEADS])
        st = sb("st", [6])
        sto = sb("sto", [TILES, 6])
        mv = sb("mv", [2])
        rt2 = sb("rt2", [4])
        mvo = sb("mvo", [TILES, 2])
        rstd = sb("rstd", [TILES])
        half = sb("half", [TILES])
        kflag = sb("kflag", [TILES])
        cols = sb("cols", [8])
        lnT = sb("lnT", [2, DEPTH])
        winT = sb("winT", [P])
        woutT = sb("woutT", [P])
        boB = sb("boB", [P])

        proj = ctx.enter_context(nc.psum_tensor("proj", [P, 2, 512], F32))
        sps = ctx.enter_context(nc.psum_tensor("sps", [P, 2, 512], F32))
        tps = ctx.enter_context(nc.psum_tensor("tps", [P, PAIRS, P], F32))
        ops = ctx.enter_context(nc.psum_tensor("ops", [P, 2, 512], F32))

        d_const = sem("d_const")
        d_w = sem("d_w")
        d_xs = [sem(f"d_xs{g}") for g in range(2)]
        d_xs2 = sem("d_xs2")
        d_vb = sem("d_vb")
        d_x = sem("d_x")
        d_out = sem("d_out")
        c_zero = sem("c_zero")
        s_idb, s_mask = sem("s_idb"), sem("s_mask")
        c_lnb = sem("c_lnb")
        c_bps, c_bp, c_w1 = sem("c_bps"), sem("c_bp"), sem("c_w1")
        c_wTp, c_wT = sem("c_wTp"), sem("c_wT")
        c_kf = sem("c_kf")
        c_sig = sem("c_sig")
        n_st, n_ag, n_eps, n_pow = sem("n_st"), sem("n_ag"), sem("n_eps"), sem("n_pow")
        n_x1, n_xn = sem("n_x1"), sem("n_xn")
        r_xTp, r_xT, r_h, r_bh, r_y, r_o, r_x2a, r_x2 = [sem(n) for n in (
            "r_xTp", "r_xT", "r_h", "r_bh", "r_y", "r_o", "r_x2a", "r_x2")]
        f_out = sem("f_out")
        p_xT, p_qT, p_kT, p_S, p_pT = sem("p_xT"), sem("p_qT"), sem("p_kT"), sem("p_S"), sem("p_pT")
        p_qkv = [sem(f"p_qkv{c}") for c in range(4)]
        p_v = [sem(f"p_v{c}") for c in range(2)]
        p_f = [sem(f"p_f{c}") for c in range(2)]
        p_O, p_oT, p_wo, p_xnT, p_hT, p_f2 = [sem(n) for n in ("p_O", "p_oT", "p_wo", "p_xnT", "p_hT", "p_f2")]
        a_xT, a_xv, a_qT, a_kT, a_pT, a_o, a_oT = [sem(n) for n in ("a_xT", "a_xv", "a_qT", "a_kT", "a_pT", "a_o", "a_oT")]
        a_cp = [sem(f"a_cp{c}") for c in range(4)]
        a_sq = [sem(f"a_sq{c}") for c in range(4)]
        a_v = [sem(f"a_v{c}") for c in range(2)]
        a_exp, a_xnT, a_hT, a_gelu = [sem(n) for n in ("a_exp", "a_xnT", "a_hT", "a_gelu")]
        v_qT, v_pT, v_car, v_bn, v_mv, v_ve, v_xn = [sem(n) for n in ("v_qT", "v_pT", "v_car", "v_bn", "v_mv", "v_ve", "v_xn")]
        v_t, v_A, v_red = [[sem(f"{n}{g}") for g in range(2)] for n in ("v_t", "v_A", "v_red")]
        v_rs = sem("v_rs")
        v_mx, v_sub, v_sum, v_rec = [sem(n) for n in ("v_mx", "v_sub", "v_sum", "v_rec")]
        v_z1, v_fa, v_fg, v_fm, v_z2a, v_z = [sem(n) for n in ("v_z1", "v_fa", "v_fg", "v_fm", "v_z2a", "v_z")]
        g_B, g_add = [[sem(f"{n}{g}") for g in range(2)] for n in ("g_B", "g_add")]
        g_tab, g_rstd, g_nrm = sem("g_tab"), sem("g_rstd"), sem("g_nrm")
        RS_STEPS = 12

        block = ctx.enter_context(nc.Block())

        class Step:

            def __init__(self, eng, h, reg, s, memo):
                self.eng, self.h, self.reg, self.s, self.memo = eng, h, reg, s, memo

            def on(self, lag):
                return self.reg is not None or 0 <= self.s - lag < N

            def val(self, key, f):
                if key not in self.memo:
                    self.memo[key] = self.eng.snap(f())
                return self.memo[key]

            def tile(self, lag):
                if self.reg is None:
                    return self.h * N + self.s - lag
                return self.reg + (self.s - lag)

            def parity(self, lag):
                return (self.s - lag) % 2

            def wait(self, sm, lag, per=1, base=0):
                if self.reg is None:
                    u = min(self.s - lag, N - 1)
                    if u < 0:
                        return
                    self.eng.wait_ge(sm, (self.h * N + u + 1) * per + base)
                elif per == 1:
                    self.eng.wait_ge(sm, self.count(lag, base))
                else:
                    c = (self.s - lag + 1) * per + base
                    self.eng.wait_ge(sm, self.val(("w", per, c), lambda: self.reg * per + c))

            def count(self, lag, base=0):
                c = self.s - lag + 1 + base
                return self.val(("w", c), lambda: self.reg + c)

            def wait_pair(self, sms, lag, per):
                if self.reg is None:
                    u = min(self.s - lag, N - 1)
                    if u >= 0:
                        self.eng.wait_ge(sms[u % 2], ((self.h * N + u) // 2 + 1) * per)
                else:
                    c = (self.s - lag) // 2 * per + per
                    self.eng.wait_ge(sms[(self.s - lag) % 2],
                                     self.val(("w", per // 2, c), lambda: self.reg * (per // 2) + c))

            def wait_within(self, sm, lag, per, n):
                c = (self.s - lag) * per + n
                if self.reg is None:
                    self.eng.wait_ge(sm, self.h * N * per + c)
                else:
                    self.eng.wait_ge(sm, self.val(("w", per, c), lambda: self.reg * per + c))

            def off(self, name, lag, f):
                if self.reg is None:
                    return f(self.tile(lag))
                return self.val((name, self.s - lag), lambda: f(self.tile(lag)))

            def slot(self, lag, back=0, part=0):
                return self.off(("slot", back, part), lag,
                                lambda u: (u % TILES + (u // POS) % 2 + 1 - back) * P + part)

            def layer(self, lag, width):
                if self.reg is None:
                    return ((self.s - lag) // TILES) * width
                return self.off(("layer", width), lag, lambda u: ((u - self.h * N) // TILES) * width)

            def layer_parity(self, lag, width):
                return self.off(("lp", width), lag, lambda u: ((u // TILES) % 2) * width)

        def pipeline(eng, h, step):
            first = h * N
            for s in range(FRONT):
                step(Step(eng, h, None, s, {}))
            with eng.Fori(first + FRONT, first + N, UNROLL) as i:
                memo = {}
                for j in range(UNROLL):
                    step(Step(eng, h, i, j, memo))
            for s in range(N, N + L_F2):
                step(Step(eng, h, None, s, {}))

        def heads(ap):
            return ap.rearrange("p (h d) -> p h d", d=DH)

        def halves(ap):
            return ap.rearrange("p (h a d) -> p h a d", a=2, d=DH // 2)


        def tiles3(ap):
            return ap.rearrange("p (t d) -> p t d", d=P)

        W_DMAS = 16 * (1 + PAIRS)
        consts = [
            (idf[:, :], c_ident), (rope[:, :], c_rope),
            (prob[:, :, :, :].rearrange("p a b c -> p (a b c)"), c_mask),
            (w1[:, :].rearrange("p (l n) -> p l n", l=DEPTH), w_1.rearrange("l p n -> p l n")),
            (bp[:, :].rearrange("p (l n) -> p l n", l=DEPTH), b_1.partition_broadcast(P)),
            (b2[:, :].rearrange("p (l n) -> p l n", l=DEPTH), b_2.partition_broadcast(P)),
            (boB[:, :], b_out.partition_broadcast(P)),
            (winT[:, :], w_in), (woutT[:, :], w_out),
            (cols[:, 0:1], b_in.rearrange("(p a) -> p a", a=1)),
            (cols[:, 1:2], a_in.rearrange("(p a) -> p a", a=1)),
            (cols[:, 2:3], b_gain.rearrange("(p a) -> p a", a=1)),
        ]
        for n in range(DEPTH):
            consts.append((lnT[:, 0, n:n + 1], ln_g[n].rearrange("(p a) -> p a", a=1)))
            consts.append((lnT[:, 1, n:n + 1], ln_b[n].rearrange("(p a) -> p a", a=1)))
        w2v = w2[:, :].rearrange("p (l c n) -> p l c n", l=DEPTH, c=3)
        for c in range(3):
            rows = min(FC, FH - c * FC)
            consts.append((w2v[0:rows, :, c, :], w_2[:, c * FC:c * FC + rows, :].rearrange("l p n -> p l n")))
        for kind, src in ((0, q_scale), (2, k_scale)):
            for l0, l1, s0, s1 in ((0, DEPTH, 0, DEPTH), (DEPTH, DEPTH + 1, 0, 1)):
                hd = DH // 2
                consts.append((scl[:, l0:l1, kind, :], src[s0:s1].partition_broadcast(P)))
                consts.append((scl[:, l0:l1, kind + 1, 0:hd], src[s0:s1, hd:DH].partition_broadcast(P)))
                consts.append((scl[:, l0:l1, kind + 1, hd:DH], src[s0:s1, 0:hd].partition_broadcast(P)))
        CONSTS = 16 * len(consts)

        @block.sync
        def _(sp):
            def load_layer(layer, parity):
                sp.dma_start(wq[:, parity, :], w_qkv[layer]).then_inc(d_w, 16)
                for c in range(PAIRS):
                    sp.dma_start(wo[:, (parity * PAIRS + c) * P:(parity * PAIRS + c + 1) * P],
                                 w_o[layer, c * P:(c + 1) * P, :]).then_inc(d_w, 16)

            def shift(k, lag, dst, sm):
                hf, cut = P // 2, P - 16
                new, tail, left = k.slot(lag), k.slot(lag, 0, hf), k.slot(lag, 1, hf)
                sp.dma_start(dst[:, 0:hf], Z[:, bass.ds(new, hf)]).then_inc(sm, 16)
                sp.dma_start(dst[1:cut + 1, hf:P], Z[0:cut, bass.ds(tail, hf)]).then_inc(sm, 16)
                sp.dma_start(dst[cut + 1:P, hf:P], Z[cut:P - 1, bass.ds(tail, hf)]).then_inc(sm, 16)
                sp.dma_start(dst[0:1, hf:P], Z[P - 1:P, bass.ds(left, hf)]).then_inc(sm, 16)

            sp.dma_start(tiles3(qk[:, :]), x_in.rearrange("b (t p) d -> p (b t) d", p=P)).then_inc(d_x, 16)
            sp.wait_ge(c_zero, 1)
            for dst, src in consts:
                sp.dma_start(dst, src).then_inc(d_const, 16)
            load_layer(0, 0)

            def step(k):
                if k.reg is not None:
                    for lag in (L_X, L_AV):
                        k.slot(lag), k.slot(lag, 0, P // 2), k.slot(lag, 1, P // 2)
                    if k.s == 0:
                        lay = k.val("w_lay", lambda: ((k.reg - k.h * N) // TILES + 1) % DEPTH)
                        at_q = k.val("w_q", lambda: ((k.reg // TILES + 1) % 2) * (3 * INNER))
                        at_o = k.val("w_o", lambda: ((k.reg // TILES + 1) % 2) * (PAIRS * P))
                if k.on(L_X):
                    k.wait(v_z, L_X, base=k.h * TILES)
                    if k.reg is None:
                        k.wait(p_xT, L_X + 2)
                    shift(k, L_X, xs[:, k.parity(L_X), :], d_xs[k.parity(L_X)])
                if k.on(L_S):
                    k.wait(a_v[1], L_S)
                    par = k.parity(L_S)
                    sp.dma_start(vb[WIN:P, :], va[0:P - WIN, par, :]).then_inc(d_vb, 16)
                    sp.dma_start(vb[0:WIN, :], va[P - WIN:P, 1 - par, :]).then_inc(d_vb, 16)
                if k.on(L_AV):
                    k.wait(v_z1, L_AV)
                    shift(k, L_AV, xs2[:, :], d_xs2)
                if k.reg is None and k.s == L_AV:
                    load_layer(1, 1)
                elif k.reg is not None and k.s == 0:
                    with sp.If(k.reg % TILES == L_AV):
                        sp.dma_start(wq[:, :, :].rearrange("p a n -> p (a n)")[:, bass.ds(at_q, 3 * INNER)],
                                     w_qkv[bass.ds(lay, 1)].rearrange("a p n -> (a p) n")).then_inc(d_w, 16)
                        for c in range(PAIRS):
                            sp.dma_start(wo[:, bass.ds(at_o + c * P, P)],
                                         w_o[bass.ds(lay, 1), c * P:(c + 1) * P, :].rearrange("a p n -> (a p) n")
                                         ).then_inc(d_w, 16)

            pipeline(sp, 0, step)
            sp.wait_ge(v_A[1], N)
            sp.wait_ge(g_B[1], N)
            sp.dma_start(tiles3(qk[:, :]), x_in.rearrange("b (t p) d -> p (b t) d", p=P)).then_inc(d_x, 16)
            sp.wait_ge(r_x2, BATCH)
            sp.dma_start(x2_dram, qk[:, :]).then_inc(d_out, 16)
            sp.wait_ge(d_out, 16)
            pipeline(sp, 1, step)
            sp.wait_ge(v_A[1], 2 * N)
            sp.wait_ge(g_B[1], 2 * N)
            sp.dma_start(qk[:, :], x2_dram).then_inc(d_x, 16)
            sp.wait_ge(f_out, 1)
            sp.dma_start(out.rearrange("b (t p) d -> p (b t) d", p=P), tiles3(rot[:, :])).then_inc(d_out, 16)
            sp.wait_ge(d_out, 32)
            sp.wait_ge(d_w, (2 * DEPTH + 1) * W_DMAS)

        @block.tensor
        def _(pe):
            mm, tr = nc.tensor.matmul, nc.tensor.transpose

            def qkv(k, c):
                w = k.layer_parity(L_QKV, 3 * INNER)
                mm(proj[:, c % 2, :], xsT[:, k.parity(L_QKV), :],
                   wq2[:, bass.ds(w + c * 512, 512)], start=True, stop=True).then_inc(p_qkv[c], 1)

            wq2 = wq[:, :, :].rearrange("p a n -> p (a n)")

            def step(k):
                if k.on(L_S):
                    k.wait(g_add[0], L_S)
                    k.wait(a_pT, L_S + 1)
                    k.wait(v_pT, L_S + 1)
                    if k.reg is None:
                        k.wait(a_xT, L_X + 1)
                    for p in range(PAIRS):
                        last = tr(tps[:, p, :], rot[:, p * P:(p + 1) * P], idf[:, :])
                    last.then_inc(p_qT, 1)
                if k.on(L_QKV):
                    if k.reg is None:
                        pe.wait_ge(d_w, (k.tile(L_QKV) // TILES + 1) * W_DMAS)
                    else:
                        pe.wait_ge(d_w, k.off("dw", L_QKV, lambda u: (u // TILES + 1) * W_DMAS))
                    k.wait(a_xT, L_QKV)
                    k.wait(a_v[0], L_S + 1)
                    qkv(k, 0)
                    k.wait(a_v[1], L_S + 1)
                    qkv(k, 1)
                if k.on(L_S):
                    k.wait(g_add[1], L_S)
                    k.wait(a_qT, L_S)
                    k.wait(v_qT, L_S)
                    for p in range(PAIRS):
                        last = tr(tps[:, p, :], rot[:, INNER + p * P:INNER + (p + 1) * P], idf[:, :])
                    last.then_inc(p_kT, 1)
                if k.on(L_AV):
                    k.wait(a_pT, L_AV)
                    k.wait(v_pT, L_AV)
                    k.wait(d_vb, L_AV, per=32)
                    k.wait(v_z1, L_AV + 1)
                    k.wait(a_hT, L_F + 1)
                    par = k.parity(L_AV)
                    for hd in range(HEADS):
                        for g in range(2):
                            v = vb[:, hd * DH:(hd + 1) * DH] if g == 0 else va[:, par, hd * DH:(hd + 1) * DH]
                            last = mm(ops[g * 64:g * 64 + 64, hd // 8, (hd % 8) * DH:(hd % 8 + 1) * DH],
                                      pTz[:, hd // 2, g * 2 + hd % 2, :, :].rearrange("p a b -> p (a b)"), v,
                                      start=True, stop=True, skip_group_check=True)
                    last.then_inc(p_O, 1)
                if k.on(L_S):
                    k.wait(v_sub, L_S + 1)
                    k.wait(a_qT, L_S)
                    k.wait(v_qT, L_S)
                    k.wait(a_kT, L_S)
                    if k.parity(L_S) == 0:
                        k.wait(v_car, L_S)
                    first = k.off("first", L_S, lambda u: ((POS - 1 - u % POS) // (POS - 1)) * 512)
                    par = k.parity(L_S)
                    for ty in range(2):
                        m = mask[:, bass.ds(first, 512)] if ty == 0 else mask[:, 0:512]
                        mm(sps[:, ty, :], idb[:, :], m, start=True, stop=False, skip_group_check=True)
                        for g in range(2):
                            w = 2 * ty + g
                            at = par * P + w * WIN
                            for p in range(PAIRS):
                                last = mm(sps[g * 64:g * 64 + 64, ty, p * 64:p * 64 + 64],
                                          qTz[:, p, w, :, :].rearrange("p a b -> p (a b)"), kT[:, p, at:at + 2 * WIN],
                                          start=False, stop=True, skip_group_check=True)
                    last.then_inc(p_S, 1)
                if k.on(L_AV):
                    k.wait(a_o, L_AV)
                    k.wait(a_kT, L_S)
                    for p in range(PAIRS):
                        last = mm(tps[:, p, :], o_sb[:, p * P:(p + 1) * P], idp[:, :], start=True, stop=True,
                                  skip_group_check=True)
                    last.then_inc(p_oT, 1)
                if k.on(L_QKV):
                    k.wait(a_sq[0], L_QKV)
                    qkv(k, 2)
                    k.wait(a_sq[1], L_QKV)
                    qkv(k, 3)
                if k.on(L_F):
                    k.wait(v_xn, L_F)
                    k.wait(a_oT, L_AV)
                    tr(tps[:, 0, :], xn[:, :], idf[:, :]).then_inc(p_xnT, 1)
                if k.on(L_X):
                    k.wait_pair(d_xs, L_X, 64)
                    k.wait(a_oT, L_AV)
                    tr(tps[:, 4, :], xs[:, k.parity(L_X), :], idf[:, :]).then_inc(p_xT, 1)
                if k.on(L_F):
                    k.wait(a_xnT, L_F)
                    at = k.layer(L_F, 2 * FH)
                    for c in range(2):
                        k.wait(a_sq[2 + c], L_QKV)
                        mm(proj[:, c, 0:FH], xnT[:, :], w1[:, bass.ds(at + c * FH, FH)],
                           start=True, stop=True).then_inc(p_f[c], 1)
                if k.on(L_S):
                    w = k.layer_parity(L_S, 3 * INNER)
                    k.wait(a_xv, L_S)
                    for c in range(2):
                        k.wait(a_sq[2 + c], L_QKV)
                        k.wait((v_fa, v_fg)[c], L_F)
                        mm(proj[:, c, :], xvT[:, k.parity(L_S), :], wq2[:, bass.ds(w + (4 + c) * 512, 512)],
                           start=True, stop=True).then_inc(p_v[c], 1)
                if k.on(L_AV):
                    k.wait(a_oT, L_AV)
                    w = k.layer_parity(L_AV, PAIRS * P)
                    for p in range(PAIRS):
                        last = mm(ops[:, 0, 0:P], oT[:, p, :],
                                  wo[:, bass.ds(w + p * P, P)], start=(p == 0), stop=(p == PAIRS - 1))
                    last.then_inc(p_wo, 1)
                if k.on(L_F2):
                    k.wait(a_hT, L_F2)
                    k.wait(a_o, L_AV)
                    at = k.layer(L_F2, 3 * P)
                    for c in range(3):
                        last = mm(ops[:, 1, 3 * P:4 * P], hT[0:FC, c, :], w2[0:FC, bass.ds(at + c * P, P)],
                                  start=(c == 0), stop=(c == 2))
                    last.then_inc(p_f2, 1)
                if k.on(L_S):
                    k.wait(g_nrm, L_S)
                    k.wait(a_xnT, L_F)
                    k.wait(a_xT, L_X)
                    k.wait(a_oT, L_AV)
                    for p in range(PAIRS):
                        last = tr(tps[:, p, :], prob[:, p, :, :].rearrange("p a b -> p (a b)"), idf[:, :])
                    last.then_inc(p_pT, 1)
                if k.on(L_F):
                    k.wait(v_fm, L_F)
                    k.wait(v_z2a, L_F2)
                    for c in range(3):
                        last = tr(ops[0:FC, 1, c * P:(c + 1) * P], hh[:, c * FC:(c + 1) * FC], idf[:, :])
                    last.then_inc(p_hT, 1)

            pe.wait_ge(d_const, CONSTS)
            tr(tps[:, 0, :], winT[:, :], idf[:, :])
            tr(tps[:, 1, :], woutT[:, :], idf[:, :]).then_inc(c_wTp, 1)
            pe.wait_ge(c_lnb, 1)
            for n in range(DEPTH):
                if n:
                    pe.wait_ge(c_bp, n)
                for c in range(2):
                    last = mm(proj[:, c, 0:FH], o_sb[:, n * P:(n + 1) * P],
                              w1[:, (2 * n + c) * FH:(2 * n + c + 1) * FH], start=True, stop=True)
                last.then_inc(c_bps, 1)
            pe.wait_ge(c_bp, DEPTH)
            pe.wait_ge(c_w1, DEPTH)
            pe.wait_ge(c_wT, 1)
            pe.wait_ge(s_idb, 1)
            pe.wait_ge(s_mask, 1)
            pe.wait_ge(c_zero, 2)
            pipeline(pe, 0, step)

            for b in range(BATCH):
                pe.wait_ge(n_xn, b + 1)
                if b:
                    pe.wait_ge(r_xT, b)
                for t in range(POS):
                    last = tr(tps[:, t, :], rot[:, (b * POS + t) * P:(b * POS + t + 1) * P], idf[:, :])
                last.then_inc(r_xTp, 1)
                pe.wait_ge(r_xT, b + 1)
                if b:
                    pe.wait_ge(r_bh, b)
                for c in range(2):
                    last = mm(proj[:, c, :], winT[:, :], sq[:, c * 512:(c + 1) * 512], start=True, stop=True)
                last.then_inc(r_h, 1)
                pe.wait_ge(r_y, b + 1)
                if b:
                    pe.wait_ge(r_x2a, b)
                for t in range(POS):
                    last = mm(sps[:, t // 4, (t % 4) * P:(t % 4 + 1) * P], o_sb[:, t * P:(t + 1) * P], woutT[:, :],
                              start=True, stop=True, skip_group_check=True)
                last.then_inc(r_o, 1)
            pe.wait_ge(r_x2a, BATCH)
            pipeline(pe, 1, step)

        @block.scalar
        def _(act):
            fn, cp = nc.scalar.activation, nc.scalar.copy

            def step(k):
                if k.on(L_AV):
                    k.wait(p_pT, L_AV)
                    k.wait(p_O, L_AV + 1)
                    cp(pTz[0:64, :, :, 0, :], tps[0:64, :, :].rearrange("p a (b c) -> p a b c", c=WIN)).then_inc(a_pT, 1)
                if k.on(L_F2):
                    k.wait(p_hT, L_F2)
                    k.wait(p_f2, L_F2 + 1)
                    cp(hT[0:FC, :, :], ops[0:FC, 1, 0:3 * P].rearrange("p (c n) -> p c n", c=3)).then_inc(a_hT, 1)
                if k.on(L_S):
                    k.wait(p_qT, L_S)
                    k.wait(p_S, L_S + 1)
                    cp(qTz[0:64, :, :, 0, :], tps[0:64, :, :].rearrange("p a (w i) -> p a w i", i=WIN)).then_inc(a_qT, 1)
                if k.on(L_QKV):
                    k.wait(v_A[0], L_ROT)
                    k.wait(g_B[0], L_ROT)
                    for c in range(2):
                        k.wait(p_qkv[c], L_QKV)
                        cp(qk[:, c * 512:(c + 1) * 512], proj[:, c, :]).then_inc(a_cp[c], 1)
                        if c == 0:
                            k.wait(v_red[1], L_ROT)
                        fn(sq[:, c * 512:(c + 1) * 512], proj[:, c, :], ACT.Square).then_inc(a_sq[c], 1)
                if k.on(L_S):
                    k.wait(p_kT, L_S)
                    k.wait(p_S, L_S + 1)
                    if k.parity(L_S) == 1:
                        k.wait(v_car, L_S + 1)
                    at = WIN + k.parity(L_S) * P
                    cp(kT[:, :, at:at + P], tps[:, :, :]).then_inc(a_kT, 1)
                if k.on(L_AV):
                    k.wait(p_O, L_AV)
                    k.wait(p_oT, L_AV + 1)
                    cp(o_sb[:, :], ops[:, :, :].rearrange("p a b -> p (a b)")).then_inc(a_o, 1)
                if k.on(L_ROT):
                    k.wait(a_xT, L_ROT)
                    k.wait(p_v[1], L_ROT + 2)
                    cp(xvT[:, k.parity(L_ROT), :], xsT[:, k.parity(L_ROT), :]).then_inc(a_xv, 1)
                if k.on(L_AV):
                    k.wait(p_oT, L_AV)
                    k.wait(p_wo, L_AV + 1)
                    cp(oT[:, :, :], tps[:, :, :]).then_inc(a_oT, 1)
                if k.on(L_QKV):
                    k.wait(v_A[1], L_ROT)
                    k.wait(g_B[1], L_ROT)
                    k.wait(v_red[0], L_QKV)
                    for c in range(2, 4):
                        k.wait(p_qkv[c], L_QKV)
                        cp(qk[:, c * 512:(c + 1) * 512], proj[:, c - 2, :]).then_inc(a_cp[c], 1)
                        fn(sq[:, (c - 2) * 512:(c - 1) * 512], proj[:, c - 2, :], ACT.Square).then_inc(a_sq[c], 1)
                if k.on(L_F):
                    k.wait(p_xnT, L_F)
                    k.wait(p_f[1], L_F + 1)
                    cp(xnT[:, :], tps[:, 0, :]).then_inc(a_xnT, 1)
                if k.on(L_X):
                    k.wait(p_xT, L_X)
                    k.wait(p_qkv[3], L_X + 2)
                    k.wait(a_xv, L_X + 2)
                    cp(xsT[:, k.parity(L_X), :], tps[:, 4, :]).then_inc(a_xT, 1)
                if k.on(L_S):
                    k.wait(v_sub, L_S)
                    fn(prob[:, :, :, :], prob[:, :, :, :], ACT.Exp).then_inc(a_exp, 1)
                if k.on(L_F):
                    k.wait(v_fg, L_F)
                    fn(fg[:, :], fg[:, :], ACT.Gelu).then_inc(a_gelu, 1)
                if k.on(L_S):
                    k.wait(p_O, L_S + 2)
                    k.wait(d_vb, L_S + 1, per=32)
                    for c in range(2):
                        k.wait(p_v[c], L_S)
                        cp(va[:, k.parity(L_S), c * 512:(c + 1) * 512], proj[:, c, :]).then_inc(a_v[c], 1)

            act.wait_ge(d_const, CONSTS)
            cp(idb[:, :], idf[:, :])
            cp(idp[:, :].rearrange("p (t g i) -> p t g i", t=2, g=2),
               idf[:, :].rearrange("p (g t i) -> p t g i", g=2, t=2)).then_inc(s_idb, 1)
            cp(mask[:, :], prob[:, :, :, :].rearrange("p a b c -> p (a b c)")).then_inc(s_mask, 1)
            act.wait_ge(c_wTp, 1)
            cp(winT[:, :], tps[:, 0, :])
            cp(woutT[:, :], tps[:, 1, :]).then_inc(c_wT, 1)
            fn(cols[:, 3:4], cols[:, 1:2], ACT.Sigmoid).then_inc(c_sig, 1)
            act.wait_ge(v_z, TILES)
            act.wait_ge(c_zero, 2)
            pipeline(act, 0, step)
            for b in range(BATCH):
                act.wait_ge(r_xTp, b + 1)
                act.wait_ge(v_red[1], N)
                if b:
                    act.wait_ge(r_h, b)
                cp(sq[:, :], tps[:, :, :].rearrange("p a b -> p (a b)")).then_inc(r_xT, 1)
            act.wait_ge(v_z, 2 * TILES + N)
            act.wait_ge(d_out, 16)
            act.wait_ge(r_h, BATCH)
            act.wait_ge(r_o, BATCH)
            pipeline(act, 1, step)

        @block.vector
        def _(dve):
            v = nc.vector

            def outer_norm(call, dst, sm):
                for t in range(TILES):
                    last = v.bn_stats(sto[:, t, :], qk[:, t * P:(t + 1) * P])
                last.then_inc(n_st, 1)
                dve.wait_ge(n_st, call)
                for t in range(TILES):
                    last = v.bn_aggr(mvo[:, t, :], sto[:, t, :])
                last.then_inc(n_ag, 1)
                dve.wait_ge(n_ag, call)
                v.tensor_scalar(rstd[:, :], mvo[:, :, 1], 1e-5, None, ALU.add).then_inc(n_eps, 1)
                dve.wait_ge(n_pow, call)
                for t in range(TILES):
                    last = v.tensor_scalar(dst(t), qk[:, t * P:(t + 1) * P], mvo[:, t, 0:1], rstd[:, t:t + 1],
                                           ALU.subtract, ALU.mult)
                    if sm is v_z:
                        last.then_inc(v_z, 1)
                    elif t % POS == POS - 1:
                        last.then_inc(sm, 1)

            def zslot(t):
                return Z[:, (t + t // POS + 1) * P:(t + t // POS + 2) * P]

            def step(k):
                if k.on(L_AV):
                    k.wait(p_pT, L_AV)
                    k.wait(p_O, L_AV + 1)
                    v.tensor_copy(pTz[64:128, :, :, 1, :],
                                  tps[64:128, :, :].rearrange("p a (b c) -> p a b c", c=WIN)).then_inc(v_pT, 1)
                if k.on(L_F):
                    k.wait(d_xs2, L_F, per=64)
                    v.bn_stats(st[:, :], xs2[:, :]).then_inc(v_bn, 1)
                if k.on(L_S) and k.parity(L_S) == 0:
                    k.wait(a_kT, L_S + 1)
                    k.wait(p_S, L_S + 1)
                    fl = k.off("flag", L_S, lambda u: u % TILES)
                    v.tensor_scalar(kT[:, :, 0:WIN], kT[:, :, 2 * P:2 * P + WIN], kflag[:, bass.ds(fl, 1)], None,
                                    ALU.mult).then_inc(v_car, 1)
                elif k.on(L_S):
                    k.wait(a_kT, L_S + 1)
                    v.tensor_copy(rt2[:, 2:3], rt2[:, 3:4]).then_inc(v_car, 1)
                if k.on(L_S):
                    k.wait(v_bn, L_F)
                    k.wait(p_qT, L_S)
                    k.wait(p_S, L_S + 1)
                    v.tensor_copy(qTz[64:128, :, :, 1, :],
                                  tps[64:128, :, :].rearrange("p a (w i) -> p a w i", i=WIN)).then_inc(v_qT, 1)
                if k.on(L_F):
                    if not k.on(L_S):
                        k.wait(v_bn, L_F)
                    v.bn_aggr(mv[:, :], st[:, :]).then_inc(v_mv, 1)
                    k.wait(v_mv, L_F)
                    v.tensor_scalar(rt2[:, 0:1], mv[:, 1:2], 1e-5, None, ALU.add).then_inc(v_ve, 1)
                if k.on(L_ROT):
                    po = k.off("pos", L_ROT, lambda u: (u % POS) * DH + ((u // TILES) % 2) * (4 * POS * DH))
                    k.wait(v_rs, L_ROT, per=RS_STEPS)
                    k.wait(g_tab, L_ROT, base=TILES - 1)
                    for g in range(2):
                        src = heads(qk[:, g * INNER:(g + 1) * INNER])
                        v.tensor_tensor(src, src, rn[:, g * HEADS:(g + 1) * HEADS].unsqueeze(2)
                                        .to_broadcast([P, HEADS, DH]), ALU.mult).then_inc(v_t[g], 1)
                        k.wait(v_t[g], L_ROT)
                        k.wait((p_qT, p_kT)[g], L_ROT + 1)
                        v.tensor_tensor(heads(rot[:, g * INNER:(g + 1) * INNER]), src,
                                        tab[:, bass.ds(po + 2 * g * POS * DH, DH)].unsqueeze(1)
                                        .to_broadcast([P, HEADS, DH]), ALU.mult).then_inc(v_A[g], 1)
                if k.on(L_F):
                    k.wait(g_rstd, L_F)
                    k.wait(p_xnT, L_F + 1)
                    v.tensor_scalar(xn[:, :], xs2[:, :], mv[:, 0:1], rt2[:, 1:2], ALU.subtract,
                                    ALU.mult).then_inc(v_xn, 1)
                if k.on(L_QKV):
                    k.wait(a_sq[1], L_QKV)
                    k.wait(v_rs, L_QKV + 1, per=RS_STEPS)
                    v.tensor_reduce(ssq[:, 0:HEADS], heads(sq[:, :]), AX, ALU.add).then_inc(v_red[0], 1)
                if k.on(L_S):
                    k.wait(p_S, L_S)
                    s4 = sps[:, :, :].rearrange("p t (a j) -> p t a j", j=2 * WIN)
                    v.tensor_reduce(mx[:, :], s4, AX, ALU.max).then_inc(v_mx, 1)
                    k.wait(v_mx, L_S)
                    k.wait(p_pT, L_S + 1)
                    v.tensor_tensor(prob[:, :, :, :].rearrange("p a t j -> p t a j"), s4,
                                    mx[:, :].rearrange("p (t a) -> p t a", t=2).unsqueeze(3)
                                    .to_broadcast([P, 2, PAIRS, 2 * WIN]), ALU.subtract).then_inc(v_sub, 1)
                if k.on(L_QKV):
                    k.wait(a_sq[3], L_QKV)
                    v.tensor_reduce(ssq[:, HEADS:2 * HEADS], heads(sq[:, :]), AX, ALU.add).then_inc(v_red[1], 1)
                if k.on(L_F):
                    at = k.layer(L_F, 2 * FH)
                    k.wait(p_f[0], L_F)
                    v.tensor_tensor(fa[:, :], proj[:, 0, 0:FH], bp[:, bass.ds(at, FH)], ALU.add).then_inc(v_fa, 1)
                    k.wait(p_f[1], L_F)
                    v.tensor_tensor(fg[:, :], proj[:, 1, 0:FH], bp[:, bass.ds(at + FH, FH)], ALU.add).then_inc(v_fg, 1)
                if k.on(L_S):
                    k.wait(a_exp, L_S)
                    v.tensor_reduce(rs[:, :], prob[:, :, :, :].rearrange("p a t j -> p (a t) j"), AX,
                                    ALU.add).then_inc(v_sum, 1)
                    k.wait(v_sum, L_S)
                    k.wait(g_nrm, L_S + 1)
                    v.reciprocal(rr[:, :], rs[:, :]).then_inc(v_rec, 1)
                if k.on(L_QKV):
                    base = {"n": 0}

                    def chain(ins):
                        ins.then_inc(v_rs, 1)
                        base["n"] += 1
                        k.wait_within(v_rs, L_QKV, RS_STEPS, base["n"])

                    k.wait(v_red[0], L_QKV)
                    k.wait(v_red[1], L_QKV)
                    k.wait(v_A[1], L_ROT)
                    chain(v.tensor_scalar(ssq[:, :], ssq[:, :], NORM_EPS2, None, ALU.max))
                    chain(v.tensor_scalar(rt[:, :].bitcast(I32), ssq[:, :].bitcast(I32), 1, None,
                                          ALU.logical_shift_right))
                    chain(v.tensor_scalar(rn[:, :].bitcast(I32), rt[:, :].bitcast(I32), -1.0, float(0x5F3759DF),
                                          ALU.mult, ALU.add))
                    for _ in range(3):
                        chain(v.tensor_tensor(rt[:, :], rn[:, :], rn[:, :], ALU.mult))
                        chain(v.scalar_tensor_tensor(out=rt[:, :], in0=rt[:, :], scalar=-0.5, in1=ssq[:, :],
                                                     op0=ALU.mult, op1=ALU.mult))
                        chain(v.scalar_tensor_tensor(out=rn[:, :], in0=rt[:, :], scalar=1.5, in1=rn[:, :],
                                                     op0=ALU.add, op1=ALU.mult))
                if k.on(L_AV):
                    k.wait(p_wo, L_AV)
                    k.wait_pair(d_xs, L_AV - 1, 64)
                    zs = Z[:, bass.ds(k.slot(L_AV), P)]
                    v.tensor_tensor(zs, zs, ops[:, 0, 0:P], ALU.add).then_inc(v_z1, 1)
                if k.on(L_F):
                    k.wait(a_gelu, L_F)
                    k.wait(p_hT, L_F + 1)
                    v.tensor_tensor(hh[:, 0:FH], fa[:, :], fg[:, :], ALU.mult).then_inc(v_fm, 1)
                if k.on(L_F2):
                    if k.reg is None:
                        k.wait(v_z, L_F2 + 1, base=(k.h + 1) * TILES)
                    k.wait(p_f2, L_F2)
                    at = k.layer(L_F2, P)
                    v.tensor_tensor(z2t[:, :], ops[:, 1, 3 * P:4 * P], b2[:, bass.ds(at, P)], ALU.add).then_inc(v_z2a, 1)
                    k.wait(v_z2a, L_F2)
                    k.wait(d_xs2, L_F2 - 1, per=64)
                    zs = Z[:, bass.ds(k.slot(L_F2), P)]
                    v.tensor_tensor(zs, zs, z2t[:, :], ALU.add).then_inc(v_z, 1)

            v.memset(w2[:, :], 0.0).then_inc(c_zero, 1)
            for ap in (Z[:, 0:P], Z[:, (POS + 1) * P:(POS + 2) * P], qTz[:, :, :, :, :], pTz[:, :, :, :, :], hh[:, :],
                       kT[:, :, :], va[:, :, :], rt2[:, :]):
                v.memset(ap, 0.0)
            v.memset(half[:, :], -0.5)
            v.memset(kflag[:, :], 1.0).then_inc(c_kf, 1)
            dve.wait_ge(c_kf, 1)
            v.memset(kflag[:, 0:1], 0.0)
            v.memset(kflag[:, POS:POS + 1], 0.0).then_inc(c_zero, 1)
            dve.wait_ge(d_x, 16)
            dve.wait_ge(c_zero, 2)
            outer_norm(1, zslot, v_z)
            dve.wait_ge(d_const, CONSTS)
            for n in range(DEPTH):
                last = v.tensor_copy(o_sb[:, n * P:(n + 1) * P], lnT[:, 1, n:n + 1].to_broadcast([P, P]))
            last.then_inc(c_lnb, 1)
            for n in range(DEPTH):
                dve.wait_ge(c_bps, n + 1)
                for c in range(2):
                    at = bp[:, (2 * n + c) * FH:(2 * n + c + 1) * FH]
                    last = v.tensor_tensor(at, at, proj[:, c, 0:FH], ALU.add)
                last.then_inc(c_bp, 1)
                at = w1[:, 2 * n * FH:2 * (n + 1) * FH]
                v.tensor_scalar(at, at, lnT[:, 0, n:n + 1], None, ALU.mult).then_inc(c_w1, 1)
            dve.wait_ge(c_bp, DEPTH)
            pipeline(dve, 0, step)

            dve.wait_ge(d_x, 32)
            dve.wait_ge(v_z, TILES + N)
            for b in range(BATCH):
                s0 = (b * (POS + 1) + 1) * P
                part = qk[:, b * INNER:(b + 1) * INNER]
                last = v.scalar_tensor_tensor(out=part, in0=Z[:, s0:s0 + POS * P], scalar=0.5, in1=part,
                                              op0=ALU.mult, op1=ALU.add)
            last.then_inc(n_x1, 1)
            dve.wait_ge(n_x1, 1)
            dve.wait_ge(p_kT, N)
            outer_norm(2, lambda t: rot[:, t * P:(t + 1) * P], n_xn)
            dve.wait_ge(g_add[1], N)
            dve.wait_ge(p_oT, N)
            dve.wait_ge(c_sig, 1)
            for b in range(BATCH):
                part = qk[:, b * INNER:(b + 1) * INNER]
                dve.wait_ge(r_h, b + 1)
                v.tensor_scalar(swp[:, :], proj[:, :, :].rearrange("p a b -> p (a b)"), cols[:, 0:1], cols[:, 2:3],
                                ALU.add, ALU.mult).then_inc(r_bh, 1)
                dve.wait_ge(r_bh, b + 1)
                if b:
                    dve.wait_ge(r_o, b)
                v.tensor_tensor_scan(o_sb[:, :], cols[:, 3:4].to_broadcast([P, SEQ]), swp[:, :], 0.0,
                                     ALU.mult, ALU.add).then_inc(r_y, 1)
                dve.wait_ge(r_o, b + 1)
                v.tensor_tensor(part, part, sps[:, :, :].rearrange("p a b -> p (a b)"), ALU.add).then_inc(r_x2a, 1)
                dve.wait_ge(r_x2a, b + 1)
                v.tensor_tensor(tiles3(part), tiles3(part), boB[:, :].unsqueeze(1).to_broadcast([P, POS, P]),
                                ALU.add).then_inc(r_x2, 1)
            dve.wait_ge(r_x2, BATCH)
            outer_norm(3, zslot, v_z)
            pipeline(dve, 1, step)
            dve.wait_ge(d_x, 48)
            dve.wait_ge(v_z, 2 * (TILES + N))
            dve.wait_ge(p_kT, 2 * N)
            for b in range(BATCH):
                s0 = (b * (POS + 1) + 1) * P
                last = v.scalar_tensor_tensor(out=rot[:, b * INNER:(b + 1) * INNER], in0=Z[:, s0:s0 + POS * P],
                                              scalar=0.5, in1=qk[:, b * INNER:(b + 1) * INNER], op0=ALU.mult,
                                              op1=ALU.add)
            last.then_inc(f_out, 1)

        @block.gpsimd
        def _(pool):
            g_ = nc.gpsimd

            def tables(k, src, dst, scale):
                g_.tensor_tensor(tab[:, bass.ds(dst, 2 * DH)].rearrange("p (a d) -> p a d", d=DH),
                                 rope[:, bass.ds(src, 2 * DH)].rearrange("p (a d) -> p a d", d=DH),
                                 scl2[:, bass.ds(scale, DH)].unsqueeze(1).to_broadcast([P, 2, DH]),
                                 ALU.mult).then_inc(g_tab, 1)

            scl2 = scl[:, :, :, :].rearrange("p l k d -> p (l k d)")

            def step(k):
                if k.on(L_F):
                    k.wait(v_ve, L_F)
                    k.wait(v_xn, L_F + 1)
                    g_.tensor_tensor(rt2[:, 1:2], rt2[:, 0:1], half[:, 0:1], ALU.pow).then_inc(g_rstd, 1)
                if k.on(L_ROT):
                    po = k.off("pos", L_ROT, lambda u: (u % POS) * DH + ((u // TILES) % 2) * (4 * POS * DH))
                    hd = DH // 2
                    for g in range(2):
                        k.wait(v_t[g], L_ROT)
                        if g == 0:
                            k.wait(g_add[1], L_ROT + 1)
                        else:
                            k.wait(g_add[0], L_ROT)
                        src = qk[:, g * INNER:(g + 1) * INNER]
                        swapped = bass.AP(src.tensor, src.offset + hd,
                                          [list(src.ap[0]), [DH, HEADS], [-hd, 2], [1, hd]])
                        t = tab[:, bass.ds(po + (2 * g + 1) * POS * DH, DH)]
                        g_.tensor_tensor(halves(swp[:, :]), swapped,
                                         t.rearrange("p (a d) -> p a d", a=2).unsqueeze(1)
                                         .to_broadcast([P, HEADS, 2, hd]), ALU.mult).then_inc(g_B[g], 1)
                        k.wait(g_B[g], L_ROT)
                        k.wait(v_A[g], L_ROT)
                        r = rot[:, g * INNER:(g + 1) * INNER]
                        g_.tensor_tensor(r, r, swp[:, :], ALU.add).then_inc(g_add[g], 1)
                    src = k.off("rsrc", L_ROT, lambda u: (u % TILES) * (2 * DH))
                    dst = k.off("rdst", L_ROT, lambda u: ((u + TILES) % (2 * TILES)) * (2 * DH))
                    sc = k.off("rscl", L_ROT, lambda u: ((u - k.h * N) // 4) * DH + 4 * DH)
                    tables(k, src, dst, sc)
                if k.on(L_S):
                    k.wait(v_rec, L_S)
                    pr = prob[:, :, :, :].rearrange("p a t j -> p (a t) j")
                    g_.tensor_tensor(pr, pr, rr[:, :].unsqueeze(2).to_broadcast([P, HEADS, 2 * WIN]),
                                     ALU.mult).then_inc(g_nrm, 1)

            def outer_pow(call):
                pool.wait_ge(n_eps, call)
                g_.tensor_tensor(rstd[:, :], rstd[:, :], half[:, :], ALU.pow).then_inc(n_pow, 1)

            pool.wait_ge(c_zero, 2)
            outer_pow(1)
            pool.wait_ge(d_const, CONSTS)
            for t in range(TILES):
                tables(None, t * 2 * DH, t * 2 * DH, (t // 4) * DH)
            pipeline(pool, 0, step)
            outer_pow(2)
            outer_pow(3)
            pipeline(pool, 1, step)


_INS = ["L0_attn_x", "L0_attn_w_in", "L0_attn_b_in", "L0_attn_a", "L0_attn_b", "L0_attn_w_out", "L0_attn_b_out",
        "L0_ffn_Wqkv", "L0_ffn_q_scale", "L0_ffn_k_scale", "L0_ffn_Wo", "L0_ffn_ln_g", "L0_ffn_ln_b",
        "L0_ffn_W1", "L0_ffn_b1", "L0_ffn_W2", "L0_ffn_b2"]


def _constants():
    f = np.float32
    half = np.arange(0, DH, 2, dtype=f)
    inv_freq = (f(1.0) / np.power(f(10000.0), half / f(DH), dtype=f)).astype(f)
    t = np.arange(SEQ, dtype=f)
    freqs = t[:, None] * inv_freq[None, :]
    freqs = np.concatenate([freqs, freqs], -1)
    base = ((half + f(0.4 * DH)) / f(1.4 * DH)).astype(f)
    scale = np.power(base[None, :], ((t - SEQ // 2) / f(WIN // 2))[:, None], dtype=f)
    scale = np.concatenate([scale, scale], -1)
    sign = np.where(np.arange(DH) < DH // 2, f(-1), f(1))
    cos, sin = np.cos(freqs), np.sin(freqs) * sign
    kinds = np.stack([cos * scale * f(QK_SCALE), sin * scale * f(QK_SCALE), cos / scale, sin / scale])
    rope = kinds.reshape(4, POS, P, DH).transpose(2, 0, 1, 3).reshape(P, 4 * POS * DH).astype(f)
    row = np.arange(P)
    i, g = (row % WIN)[:, None], (row // (2 * WIN))[:, None]
    j = (np.arange(512) % (2 * WIN))[None, :]
    usual = ((j < WIN) & (j >= i)) | ((j >= WIN) & (j - WIN <= i))
    first = np.where(g == 0, usual & (j >= WIN), usual)
    mask = np.concatenate([np.where(m, 0.0, NEG) for m in (usual, first)], 1).astype(f)
    return {"rope": rope, "mask": mask, "ident": np.eye(P, dtype=f)}


def kernel(**inputs):
    import concourse.bacc as _bacc
    from concourse.bass_utils import run_bass_kernel_spmd as _run

    nc = _bacc.Bacc("TRN2", target_bir_lowering=False, num_devices=1)
    arrays, args = {}, []
    for name in _INS:
        a = np.ascontiguousarray(inputs[name])
        arrays[f"in_{name}"] = a
        args.append(nc.dram_tensor(f"in_{name}", a.shape, mybir.dt.from_np(a.dtype), kind="ExternalInput").ap())
    for name, a in _constants().items():
        arrays[f"const_{name}"] = a
        args.append(nc.dram_tensor(f"const_{name}", a.shape, mybir.dt.from_np(a.dtype), kind="ExternalInput").ap())
    x2 = nc.dram_tensor("x2_scratch", (P, TILES * P), F32).ap()
    out = nc.dram_tensor("out_0", (BATCH, SEQ, P), F32, kind="ExternalOutput").ap()
    macaron(nc, *args, x2, out)
    r = _run(nc, [arrays], core_ids=[0])
    return r.results[0]["out_0"]
```

```python
from contextlib import ExitStack

import numpy as np

import concourse.bass as bass
from concourse import mybir

F32 = mybir.dt.float32
BF16 = mybir.dt.bfloat16
I32 = mybir.dt.int32
ALU = mybir.AluOpType
ACT = mybir.ActivationFunctionType
AX = mybir.AxisListType.X

P = 128
DEPTH, HEADS, DH, WIN = 6, 16, 64, 32
BATCH, SEQ = 2, 1024
INNER = HEADS * DH
PAIRS = HEADS // 2
POS = SEQ // P
TILES = BATCH * POS
N = DEPTH * TILES
SLOTS = BATCH * (POS + 1)
FH = P * 4 * 2 // 3
FC = (FH + 2) // 3
QK_SCALE = 8.0
NEG = -1.0e30
NORM_EPS2 = 1e-24

L_X, L_QKV, L_S, L_AV, L_WO, L_F, L_F2 = 0, 1, 2, 3, 4, 5, 6
FRONT = 6
UNROLL = 2


def macaron(nc, x_in, w_in, b_in, a_in, b_gain, w_out, b_out, w_qkv, q_scale, k_scale, w_o,
            ln_g, ln_b, w_1, b_1, w_2, b_2, c_rope, c_mask, c_ident, x2_dram, out):
    with ExitStack() as ctx:
        def sb(name, shape, dt=F32):
            return ctx.enter_context(nc.sbuf_tensor(name, [P] + shape, dt))

        def sem(name):
            return ctx.enter_context(nc.semaphore(name))

        Z = sb("Z", [SLOTS * P])
        qk = sb("qk", [2 * INNER])
        rot = sb("rot", [2 * INNER])
        swp = sb("swp", [INNER])
        sq = sb("sq", [INNER])
        kT = sb("kT", [PAIRS, WIN + 2 * P])
        qTz = sb("qTz", [PAIRS, 4, 2, WIN])
        prob = sb("prob", [PAIRS, 2, 2 * WIN])
        pTz = sb("pTz", [PAIRS, 4, 2, WIN])
        oT = sb("oT", [PAIRS, P])
        va = sb("va", [2, INNER])
        vb = sb("vb", [INNER])
        wq = sb("wq", [2, 3 * INNER])
        wo = sb("wo", [2 * PAIRS * P])
        tab = sb("tab", [2 * 4 * POS * DH])
        rope = sb("rope", [4 * POS * DH])
        scl = sb("scl", [DEPTH + 1, 4, DH])
        w1 = sb("w1", [DEPTH * 2 * FH])
        w2 = sb("w2", [DEPTH * 3 * P])
        bp = sb("bp", [DEPTH * 2 * FH])
        b2 = sb("b2", [DEPTH * P])
        mask = sb("mask", [2 * 512], BF16)
        idf = sb("idf", [P])
        idb = sb("idb", [P], BF16)
        xs = sb("xs", [2, P])
        xsT = sb("xsT", [2, P])
        xs2 = sb("xs2", [P])
        xn = sb("xn", [P])
        xnT = sb("xnT", [P])
        fa = sb("fa", [FH])
        fg = sb("fg", [FH])
        hh = sb("hh", [3 * FC])
        hT = sb("hT", [3, P])
        z2t = sb("z2t", [P])
        ssq = sb("ssq", [2 * HEADS])
        rn = sb("rn", [2 * HEADS])
        rt = sb("rt", [2 * HEADS])
        mx = sb("mx", [HEADS])
        rs = sb("rs", [HEADS])
        rr = sb("rr", [HEADS])
        st = sb("st", [6])
        sto = sb("sto", [TILES, 6])
        mv = sb("mv", [2])
        rt2 = sb("rt2", [4])
        mvo = sb("mvo", [TILES, 2])
        rstd = sb("rstd", [TILES])
        half = sb("half", [TILES])
        kflag = sb("kflag", [TILES])
        cols = sb("cols", [8])
        lnT = sb("lnT", [2, DEPTH])
        winT = sb("winT", [P])
        woutT = sb("woutT", [P])
        boB = sb("boB", [P])

        proj = ctx.enter_context(nc.psum_tensor("proj", [P, 2, 512], F32))
        sps = ctx.enter_context(nc.psum_tensor("sps", [P, 2, 512], F32))
        tps = ctx.enter_context(nc.psum_tensor("tps", [P, PAIRS, P], F32))
        ops = ctx.enter_context(nc.psum_tensor("ops", [P, 2, 512], F32))

        d_const = sem("d_const")
        d_w = sem("d_w")
        d_xs = [sem(f"d_xs{g}") for g in range(2)]
        d_xs2 = sem("d_xs2")
        d_vb = sem("d_vb")
        d_x = sem("d_x")
        d_out = sem("d_out")
        c_zero = sem("c_zero")
        s_idb, s_mask = sem("s_idb"), sem("s_mask")
        c_lnb = sem("c_lnb")
        c_bps, c_bp, c_w1 = sem("c_bps"), sem("c_bp"), sem("c_w1")
        c_wTp, c_wT = sem("c_wTp"), sem("c_wT")
        c_kf = sem("c_kf")
        c_sig = sem("c_sig")
        n_st, n_ag, n_eps, n_pow = sem("n_st"), sem("n_ag"), sem("n_eps"), sem("n_pow")
        n_x1, n_xn = sem("n_x1"), sem("n_xn")
        r_xTp, r_xT, r_h, r_bh, r_y, r_o, r_x2a, r_x2 = [sem(n) for n in (
            "r_xTp", "r_xT", "r_h", "r_bh", "r_y", "r_o", "r_x2a", "r_x2")]
        f_out = sem("f_out")
        p_xT, p_qT, p_kT, p_S, p_pT = sem("p_xT"), sem("p_qT"), sem("p_kT"), sem("p_S"), sem("p_pT")
        p_qkv = [sem(f"p_qkv{c}") for c in range(4)]
        p_v = [sem(f"p_v{c}") for c in range(2)]
        p_f = [sem(f"p_f{c}") for c in range(2)]
        p_O, p_wo, p_xnT, p_hT, p_f2 = [sem(n) for n in ("p_O", "p_wo", "p_xnT", "p_hT", "p_f2")]
        a_xT, a_qT, a_kT, a_pT, a_oT = [sem(n) for n in ("a_xT", "a_qT", "a_kT", "a_pT", "a_oT")]
        a_cp = [sem(f"a_cp{c}") for c in range(4)]
        a_sq = [sem(f"a_sq{c}") for c in range(4)]
        a_v = [sem(f"a_v{c}") for c in range(2)]
        a_exp, a_xnT, a_hT, a_gelu = [sem(n) for n in ("a_exp", "a_xnT", "a_hT", "a_gelu")]
        v_qT, v_car, v_bn, v_mv, v_ve, v_xn = [sem(n) for n in ("v_qT", "v_car", "v_bn", "v_mv", "v_ve", "v_xn")]
        v_t, v_A, v_red = [[sem(f"{n}{g}") for g in range(2)] for n in ("v_t", "v_A", "v_red")]
        v_rs = sem("v_rs")
        v_mx, v_sub, v_sum, v_rec = [sem(n) for n in ("v_mx", "v_sub", "v_sum", "v_rec")]
        v_z1, v_fa, v_fg, v_fm, v_z2a, v_z = [sem(n) for n in ("v_z1", "v_fa", "v_fg", "v_fm", "v_z2a", "v_z")]
        g_B, g_add = [[sem(f"{n}{g}") for g in range(2)] for n in ("g_B", "g_add")]
        g_tab, g_rstd, g_nrm = sem("g_tab"), sem("g_rstd"), sem("g_nrm")
        RS_STEPS = 12

        block = ctx.enter_context(nc.Block())

        class Step:

            def __init__(self, eng, h, reg, s, memo):
                self.eng, self.h, self.reg, self.s, self.memo = eng, h, reg, s, memo

            def on(self, lag):
                return self.reg is not None or 0 <= self.s - lag < N

            def val(self, key, f):
                if key not in self.memo:
                    self.memo[key] = self.eng.snap(f())
                return self.memo[key]

            def tile(self, lag):
                if self.reg is None:
                    return self.h * N + self.s - lag
                return self.reg + (self.s - lag)

            def parity(self, lag):
                return (self.s - lag) % 2

            def wait(self, sm, lag, per=1, base=0):
                if self.reg is None:
                    u = min(self.s - lag, N - 1)
                    if u < 0:
                        return
                    self.eng.wait_ge(sm, (self.h * N + u + 1) * per + base)
                elif per == 1:
                    self.eng.wait_ge(sm, self.count(lag, base))
                else:
                    c = (self.s - lag + 1) * per + base
                    self.eng.wait_ge(sm, self.val(("w", per, c), lambda: self.reg * per + c))

            def count(self, lag, base=0):
                c = self.s - lag + 1 + base
                return self.val(("w", c), lambda: self.reg + c)

            def wait_pair(self, sms, lag, per):
                if self.reg is None:
                    u = min(self.s - lag, N - 1)
                    if u >= 0:
                        self.eng.wait_ge(sms[u % 2], ((self.h * N + u) // 2 + 1) * per)
                else:
                    c = (self.s - lag) // 2 * per + per
                    self.eng.wait_ge(sms[(self.s - lag) % 2],
                                     self.val(("w", per // 2, c), lambda: self.reg * (per // 2) + c))

            def wait_even(self, sm, lag):
                if self.reg is None:
                    u = self.s - lag
                    if u >= 0:
                        self.eng.wait_ge(sm, (self.h * N + u) // 2 + 1)
                else:
                    c = (self.s - lag) // 2 + 1
                    self.eng.wait_ge(sm, self.val(("even", c), lambda: self.reg // 2 + c))

            def wait_within(self, sm, lag, per, n):
                c = (self.s - lag) * per + n
                if self.reg is None:
                    self.eng.wait_ge(sm, self.h * N * per + c)
                else:
                    self.eng.wait_ge(sm, self.val(("w", per, c), lambda: self.reg * per + c))

            def off(self, name, lag, f):
                if self.reg is None:
                    return f(self.tile(lag))
                return self.val((name, self.s - lag), lambda: f(self.tile(lag)))

            def slot(self, lag, back=0, part=0):
                return self.off(("slot", back, part), lag,
                                lambda u: (u % TILES + (u // POS) % 2 + 1 - back) * P + part)

            def layer(self, lag, width):
                if self.reg is None:
                    return ((self.s - lag) // TILES) * width
                return self.off(("layer", width), lag, lambda u: ((u - self.h * N) // TILES) * width)

            def layer_parity(self, lag, width):
                return self.off(("lp", width), lag, lambda u: ((u // TILES) % 2) * width)

        def pipeline(eng, h, step):
            first = h * N
            for s in range(FRONT):
                step(Step(eng, h, None, s, {}))
            with eng.Fori(first + FRONT, first + N, UNROLL) as i:
                memo = {}
                for j in range(UNROLL):
                    step(Step(eng, h, i, j, memo))
            for s in range(N, N + L_F2):
                step(Step(eng, h, None, s, {}))

        def heads(ap):
            return ap.rearrange("p (h d) -> p h d", d=DH)

        def halves(ap):
            return ap.rearrange("p (h a d) -> p h a d", a=2, d=DH // 2)


        def tiles3(ap):
            return ap.rearrange("p (t d) -> p t d", d=P)

        W_DMAS = 16 * (1 + PAIRS)
        consts = [
            (idf[:, :], c_ident), (rope[:, :], c_rope),
            (prob[:, :, :, :].rearrange("p a b c -> p (a b c)"), c_mask),
            (w1[:, :].rearrange("p (l n) -> p l n", l=DEPTH), w_1.rearrange("l p n -> p l n")),
            (bp[:, :].rearrange("p (l n) -> p l n", l=DEPTH), b_1.partition_broadcast(P)),
            (b2[:, :].rearrange("p (l n) -> p l n", l=DEPTH), b_2.partition_broadcast(P)),
            (boB[:, :], b_out.partition_broadcast(P)),
            (winT[:, :], w_in), (woutT[:, :], w_out),
            (cols[:, 0:1], b_in.rearrange("(p a) -> p a", a=1)),
            (cols[:, 1:2], a_in.rearrange("(p a) -> p a", a=1)),
            (cols[:, 2:3], b_gain.rearrange("(p a) -> p a", a=1)),
        ]
        for n in range(DEPTH):
            consts.append((lnT[:, 0, n:n + 1], ln_g[n].rearrange("(p a) -> p a", a=1)))
            consts.append((lnT[:, 1, n:n + 1], ln_b[n].rearrange("(p a) -> p a", a=1)))
        w2v = w2[:, :].rearrange("p (l c n) -> p l c n", l=DEPTH, c=3)
        for c in range(3):
            rows = min(FC, FH - c * FC)
            consts.append((w2v[0:rows, :, c, :], w_2[:, c * FC:c * FC + rows, :].rearrange("l p n -> p l n")))
        for kind, src in ((0, q_scale), (2, k_scale)):
            for l0, l1, s0, s1 in ((0, DEPTH, 0, DEPTH), (DEPTH, DEPTH + 1, 0, 1)):
                hd = DH // 2
                consts.append((scl[:, l0:l1, kind, :], src[s0:s1].partition_broadcast(P)))
                consts.append((scl[:, l0:l1, kind + 1, 0:hd], src[s0:s1, hd:DH].partition_broadcast(P)))
                consts.append((scl[:, l0:l1, kind + 1, hd:DH], src[s0:s1, 0:hd].partition_broadcast(P)))
        CONSTS = 16 * len(consts)

        @block.sync
        def _(sp):
            def load_layer(layer, parity):
                sp.dma_start(wq[:, parity, :], w_qkv[layer]).then_inc(d_w, 16)
                for c in range(PAIRS):
                    sp.dma_start(wo[:, (parity * PAIRS + c) * P:(parity * PAIRS + c + 1) * P],
                                 w_o[layer, c * P:(c + 1) * P, :]).then_inc(d_w, 16)

            def shift(k, lag, dst, sm):
                hf, cut = P // 2, P - 16
                new, tail, left = k.slot(lag), k.slot(lag, 0, hf), k.slot(lag, 1, hf)
                sp.dma_start(dst[:, 0:hf], Z[:, bass.ds(new, hf)]).then_inc(sm, 16)
                sp.dma_start(dst[1:cut + 1, hf:P], Z[0:cut, bass.ds(tail, hf)]).then_inc(sm, 16)
                sp.dma_start(dst[cut + 1:P, hf:P], Z[cut:P - 1, bass.ds(tail, hf)]).then_inc(sm, 16)
                sp.dma_start(dst[0:1, hf:P], Z[P - 1:P, bass.ds(left, hf)]).then_inc(sm, 16)

            sp.dma_start(tiles3(qk[:, :]), x_in.rearrange("b (t p) d -> p (b t) d", p=P)).then_inc(d_x, 16)
            sp.wait_ge(c_zero, 1)
            for dst, src in consts:
                sp.dma_start(dst, src).then_inc(d_const, 16)
            load_layer(0, 0)

            def step(k):
                if k.reg is not None:
                    for lag in (L_X, L_WO):
                        k.slot(lag), k.slot(lag, 0, P // 2), k.slot(lag, 1, P // 2)
                    if k.s == 0:
                        lay = k.val("w_lay", lambda: ((k.reg - k.h * N) // TILES + 1) % DEPTH)
                        at_q = k.val("w_q", lambda: ((k.reg // TILES + 1) % 2) * (3 * INNER))
                        at_o = k.val("w_o", lambda: ((k.reg // TILES + 1) % 2) * (PAIRS * P))
                if k.on(L_X):
                    k.wait(v_z, L_X, base=k.h * TILES)
                    if k.reg is None:
                        k.wait(p_xT, L_X + 2)
                    shift(k, L_X, xs[:, k.parity(L_X), :], d_xs[k.parity(L_X)])
                if k.on(L_WO):
                    k.wait(v_z1, L_WO)
                    shift(k, L_WO, xs2[:, :], d_xs2)
                if k.reg is None and k.s == L_WO:
                    load_layer(1, 1)
                elif k.reg is not None and k.s == 0:
                    with sp.If(k.reg % TILES == L_WO):
                        sp.dma_start(wq[:, :, :].rearrange("p a n -> p (a n)")[:, bass.ds(at_q, 3 * INNER)],
                                     w_qkv[bass.ds(lay, 1)].rearrange("a p n -> (a p) n")).then_inc(d_w, 16)
                        for c in range(PAIRS):
                            sp.dma_start(wo[:, bass.ds(at_o + c * P, P)],
                                         w_o[bass.ds(lay, 1), c * P:(c + 1) * P, :].rearrange("a p n -> (a p) n")
                                         ).then_inc(d_w, 16)

                if k.on(L_S):
                    k.wait(a_v[1], L_S)
                    par = k.parity(L_S)
                    sp.dma_start(vb[WIN:P, :], va[0:P - WIN, par, :]).then_inc(d_vb, 16)
                    sp.dma_start(vb[0:WIN, :], va[P - WIN:P, 1 - par, :]).then_inc(d_vb, 16)

            pipeline(sp, 0, step)
            sp.wait_ge(v_A[1], N)
            sp.wait_ge(g_B[1], N)
            sp.dma_start(tiles3(qk[:, :]), x_in.rearrange("b (t p) d -> p (b t) d", p=P)).then_inc(d_x, 16)
            sp.wait_ge(r_x2, BATCH)
            sp.dma_start(x2_dram, qk[:, :]).then_inc(d_out, 16)
            sp.wait_ge(d_out, 16)
            pipeline(sp, 1, step)
            sp.wait_ge(v_A[1], 2 * N)
            sp.wait_ge(g_B[1], 2 * N)
            sp.dma_start(qk[:, :], x2_dram).then_inc(d_x, 16)
            sp.wait_ge(f_out, 1)
            sp.dma_start(out.rearrange("b (t p) d -> p (b t) d", p=P), tiles3(rot[:, :])).then_inc(d_out, 16)
            sp.wait_ge(d_out, 32)
            sp.wait_ge(d_w, (2 * DEPTH + 1) * W_DMAS)

        @block.tensor
        def _(pe):
            mm, tr = nc.tensor.matmul, nc.tensor.transpose

            def qkv(k, c):
                w = k.layer_parity(L_QKV, 3 * INNER)
                mm(proj[:, c % 2, :], xsT[:, k.parity(L_QKV), :],
                   wq2[:, bass.ds(w + c * 512, 512)], start=True, stop=True).then_inc(p_qkv[c], 1)

            wq2 = wq[:, :, :].rearrange("p a n -> p (a n)")

            def step(k):
                if k.on(L_QKV):
                    if k.reg is None:
                        pe.wait_ge(d_w, (k.tile(L_QKV) // TILES + 1) * W_DMAS)
                    else:
                        pe.wait_ge(d_w, k.off("dw", L_QKV, lambda u: (u // TILES + 1) * W_DMAS))
                    k.wait(a_xT, L_QKV)
                    k.wait(a_v[0], L_S + 1)
                    qkv(k, 0)
                    k.wait(a_v[1], L_S + 1)
                    qkv(k, 1)
                if k.on(L_WO):
                    k.wait(a_oT, L_WO)
                    w = k.layer_parity(L_WO, PAIRS * P)
                    for p in range(PAIRS):
                        last = mm(ops[:, 0, 0:P], oT[:, p, :], wo[:, bass.ds(w + p * P, P)], start=(p == 0),
                                  stop=(p == PAIRS - 1))
                    last.then_inc(p_wo, 1)
                if k.on(L_F2):
                    k.wait(a_hT, L_F2)
                    at = k.layer(L_F2, 3 * P)
                    for c in range(3):
                        last = mm(ops[:, 1, 3 * P:4 * P], hT[0:FC, c, :], w2[0:FC, bass.ds(at + c * P, P)],
                                  start=(c == 0), stop=(c == 2))
                    last.then_inc(p_f2, 1)
                if k.on(L_S):
                    k.wait(g_add[0], L_S)
                    k.wait(a_xnT, L_F)
                    for p in range(PAIRS):
                        last = tr(tps[:, p, :], rot[:, p * P:(p + 1) * P], idf[:, :])
                    last.then_inc(p_qT, 1)
                if k.on(L_QKV):
                    k.wait(a_sq[0], L_QKV)
                    qkv(k, 2)
                    k.wait(a_sq[1], L_QKV)
                    qkv(k, 3)
                if k.on(L_AV):
                    k.wait(g_nrm, L_AV)
                    k.wait(a_qT, L_S)
                    k.wait(v_qT, L_S)
                    k.wait(a_xnT, L_F)
                    for p in range(PAIRS):
                        last = tr(tps[:, p, :], prob[:, p, :, :].rearrange("p a b -> p (a b)"), idf[:, :])
                    last.then_inc(p_pT, 1)
                if k.on(L_F):
                    k.wait(a_xnT, L_F)
                    at = k.layer(L_F, 2 * FH)
                    for c in range(2):
                        k.wait(a_sq[2 + c], L_QKV)
                        mm(proj[:, c, 0:FH], xnT[:, :], w1[:, bass.ds(at + c * FH, FH)],
                           start=True, stop=True).then_inc(p_f[c], 1)
                if k.on(L_S):
                    k.wait(g_add[1], L_S)
                    k.wait(a_pT, L_AV)
                    k.wait(a_qT, L_S)
                    k.wait(v_qT, L_S)
                    for p in range(PAIRS):
                        last = tr(tps[:, p, :], rot[:, INNER + p * P:INNER + (p + 1) * P], idf[:, :])
                    last.then_inc(p_kT, 1)
                if k.on(L_AV):
                    k.wait(a_pT, L_AV)
                    k.wait(d_vb, L_AV, per=32)
                    k.wait(v_z1, L_WO)
                    k.wait(v_z2a, L_F2)
                    par = k.parity(L_AV)
                    for p in range(PAIRS):
                        o4 = ops[:, p // 4, (p % 4) * P:(p % 4 + 1) * P].rearrange("p (t g i) -> p t g i", t=2, g=2)
                        for g in range(2):
                            for hp in range(2):
                                at = (2 * p + hp) * DH
                                v = vb[:, at:at + DH] if g == 0 else va[:, par, at:at + DH]
                                last = mm(o4[hp * DH:(hp + 1) * DH, :, g, :], v,
                                          pTz[:, p, g * 2 + hp, :, :].rearrange("p a b -> p (a b)"),
                                          start=True, stop=True, skip_group_check=True)
                    last.then_inc(p_O, 1)
                if k.on(L_S):
                    k.wait(v_sub, L_S + 1)
                    k.wait(a_qT, L_S)
                    k.wait(v_qT, L_S)
                    k.wait(a_kT, L_S)
                    if k.parity(L_S) == 0:
                        k.wait_even(v_car, L_S)
                    first = k.off("first", L_S, lambda u: ((POS - 1 - u % POS) // (POS - 1)) * 512)
                    par = k.parity(L_S)
                    for ty in range(2):
                        m = mask[:, bass.ds(first, 512)] if ty == 0 else mask[:, 0:512]
                        mm(sps[:, ty, :], idb[:, :], m, start=True, stop=False, skip_group_check=True)
                        for p in range(PAIRS):
                            for g in range(2):
                                w = 2 * ty + g
                                at = par * P + w * WIN
                                last = mm(sps[g * 64:g * 64 + 64, ty, p * 64:p * 64 + 64],
                                          qTz[:, p, w, :, :].rearrange("p a b -> p (a b)"), kT[:, p, at:at + 2 * WIN],
                                          start=False, stop=True, skip_group_check=True)
                    last.then_inc(p_S, 1)
                    w = k.layer_parity(L_S, 3 * INNER)
                    for c in range(2):
                        k.wait(a_sq[2 + c], L_QKV)
                        k.wait((v_fa, v_fg)[c], L_F)
                        mm(proj[:, c, :], xsT[:, k.parity(L_S), :], wq2[:, bass.ds(w + (4 + c) * 512, 512)],
                           start=True, stop=True).then_inc(p_v[c], 1)
                if k.on(L_WO):
                    k.wait(v_xn, L_WO)
                    k.wait(a_kT, L_S)
                    tr(tps[:, 0, :], xn[:, :], idf[:, :]).then_inc(p_xnT, 1)
                if k.on(L_X):
                    k.wait_pair(d_xs, L_X, 64)
                    k.wait(a_kT, L_S)
                    tr(tps[:, 4, :], xs[:, k.parity(L_X), :], idf[:, :]).then_inc(p_xT, 1)
                if k.on(L_F):
                    k.wait(v_fm, L_F)
                    k.wait(a_oT, L_AV)
                    for c in range(3):
                        last = tr(ops[0:FC, 1, c * P:(c + 1) * P], hh[:, c * FC:(c + 1) * FC], idf[:, :])
                    last.then_inc(p_hT, 1)

            pe.wait_ge(d_const, CONSTS)
            tr(tps[:, 0, :], winT[:, :], idf[:, :])
            tr(tps[:, 1, :], woutT[:, :], idf[:, :]).then_inc(c_wTp, 1)
            pe.wait_ge(c_lnb, 1)
            for n in range(DEPTH):
                if n:
                    pe.wait_ge(c_bp, n)
                for c in range(2):
                    last = mm(proj[:, c, 0:FH], rot[:, n * P:(n + 1) * P],
                              w1[:, (2 * n + c) * FH:(2 * n + c + 1) * FH], start=True, stop=True)
                last.then_inc(c_bps, 1)
            pe.wait_ge(c_bp, DEPTH)
            pe.wait_ge(c_w1, DEPTH)
            pe.wait_ge(c_wT, 1)
            pe.wait_ge(s_idb, 1)
            pe.wait_ge(s_mask, 1)
            pe.wait_ge(c_zero, 2)
            pipeline(pe, 0, step)

            for b in range(BATCH):
                pe.wait_ge(n_xn, b + 1)
                if b:
                    pe.wait_ge(r_xT, b)
                for t in range(POS):
                    last = tr(tps[:, t, :], rot[:, (b * POS + t) * P:(b * POS + t + 1) * P], idf[:, :])
                last.then_inc(r_xTp, 1)
                pe.wait_ge(r_xT, b + 1)
                if b:
                    pe.wait_ge(r_bh, b)
                for c in range(2):
                    last = mm(proj[:, c, :], winT[:, :], sq[:, c * 512:(c + 1) * 512], start=True, stop=True)
                last.then_inc(r_h, 1)
                pe.wait_ge(r_y, b + 1)
                if b:
                    pe.wait_ge(r_x2a, b)
                for t in range(POS):
                    last = mm(sps[:, t // 4, (t % 4) * P:(t % 4 + 1) * P], oT[:, t, :], woutT[:, :],
                              start=True, stop=True, skip_group_check=True)
                last.then_inc(r_o, 1)
            pe.wait_ge(r_x2a, BATCH)
            pipeline(pe, 1, step)

        @block.scalar
        def _(act):
            fn, cp = nc.scalar.activation, nc.scalar.copy

            def step(k):
                if k.on(L_AV):
                    k.wait(v_sub, L_AV)
                    fn(prob[:, :, :, :], prob[:, :, :, :], ACT.Exp).then_inc(a_exp, 1)
                if k.on(L_QKV):
                    k.wait(v_A[0], L_QKV + 1)
                    k.wait(g_B[0], L_QKV + 1)
                    for c in range(2):
                        k.wait(p_qkv[c], L_QKV)
                        cp(qk[:, c * 512:(c + 1) * 512], proj[:, c, :]).then_inc(a_cp[c], 1)
                        if c == 0:
                            k.wait(v_red[1], L_QKV + 1)
                        fn(sq[:, c * 512:(c + 1) * 512], proj[:, c, :], ACT.Square).then_inc(a_sq[c], 1)
                if k.on(L_S):
                    k.wait(p_qT, L_S)
                    k.wait(p_S, L_S + 1)
                    cp(qTz[0:64, :, :, 0, :], tps[0:64, :, :].rearrange("p a (w i) -> p a w i", i=WIN)).then_inc(a_qT, 1)
                if k.on(L_QKV):
                    k.wait(v_A[1], L_QKV + 1)
                    k.wait(g_B[1], L_QKV + 1)
                    k.wait(v_red[0], L_QKV)
                    for c in range(2, 4):
                        k.wait(p_qkv[c], L_QKV)
                        cp(qk[:, c * 512:(c + 1) * 512], proj[:, c - 2, :]).then_inc(a_cp[c], 1)
                        fn(sq[:, (c - 2) * 512:(c - 1) * 512], proj[:, c - 2, :], ACT.Square).then_inc(a_sq[c], 1)
                if k.on(L_AV):
                    k.wait(p_pT, L_AV)
                    k.wait(p_O, L_AV + 1)
                    for t in range(2):
                        rows = slice(t * 64, t * 64 + 64)
                        last = cp(pTz[rows, :, :, t, :], tps[rows, :, :].rearrange("p a (b c) -> p a b c", c=WIN))
                    last.then_inc(a_pT, 1)
                if k.on(L_S):
                    k.wait(p_kT, L_S)
                    k.wait(p_S, L_S + 1)
                    if k.parity(L_S) == 1:
                        k.wait_even(v_car, L_S + 1)
                    at = WIN + k.parity(L_S) * P
                    cp(kT[:, :, at:at + P], tps[:, :, :]).then_inc(a_kT, 1)
                if k.on(L_F):
                    k.wait(v_fg, L_F)
                    fn(fg[:, :], fg[:, :], ACT.Gelu).then_inc(a_gelu, 1)
                if k.on(L_AV):
                    k.wait(p_O, L_AV)
                    k.wait(p_wo, L_AV + 1)
                    cp(oT[:, :, :].rearrange("p a b -> p (a b)"), ops[:, :, :].rearrange("p a b -> p (a b)")).then_inc(a_oT, 1)
                if k.on(L_S):
                    k.wait(p_O, L_S + 2)
                    k.wait(d_vb, L_S + 1, per=32)
                    for c in range(2):
                        k.wait(p_v[c], L_S)
                        cp(va[:, k.parity(L_S), c * 512:(c + 1) * 512], proj[:, c, :]).then_inc(a_v[c], 1)
                if k.on(L_WO):
                    k.wait(p_xnT, L_WO)
                    k.wait(p_f[1], L_WO + 1)
                    cp(xnT[:, :], tps[:, 0, :]).then_inc(a_xnT, 1)
                if k.on(L_X):
                    k.wait(p_xT, L_X)
                    k.wait(p_v[1], L_X + 2)
                    cp(xsT[:, k.parity(L_X), :], tps[:, 4, :]).then_inc(a_xT, 1)
                if k.on(L_F):
                    k.wait(p_hT, L_F)
                    k.wait(p_f2, L_F + 1)
                    cp(hT[0:FC, :, :], ops[0:FC, 1, 0:3 * P].rearrange("p (c n) -> p c n", c=3)).then_inc(a_hT, 1)

            act.wait_ge(d_const, CONSTS)
            cp(idb[:, :], idf[:, :]).then_inc(s_idb, 1)
            cp(mask[:, :], prob[:, :, :, :].rearrange("p a b c -> p (a b c)")).then_inc(s_mask, 1)
            act.wait_ge(c_wTp, 1)
            cp(winT[:, :], tps[:, 0, :])
            cp(woutT[:, :], tps[:, 1, :]).then_inc(c_wT, 1)
            fn(cols[:, 3:4], cols[:, 1:2], ACT.Sigmoid).then_inc(c_sig, 1)
            act.wait_ge(v_z, TILES)
            act.wait_ge(c_zero, 2)
            pipeline(act, 0, step)
            for b in range(BATCH):
                act.wait_ge(r_xTp, b + 1)
                act.wait_ge(v_red[1], N)
                if b:
                    act.wait_ge(r_h, b)
                cp(sq[:, :], tps[:, :, :].rearrange("p a b -> p (a b)")).then_inc(r_xT, 1)
            act.wait_ge(v_z, 2 * TILES + N)
            act.wait_ge(d_out, 16)
            act.wait_ge(r_h, BATCH)
            act.wait_ge(r_o, BATCH)
            pipeline(act, 1, step)

        @block.vector
        def _(dve):
            v = nc.vector

            def outer_norm(call, dst, sm):
                for t in range(TILES):
                    last = v.bn_stats(sto[:, t, :], qk[:, t * P:(t + 1) * P])
                last.then_inc(n_st, 1)
                dve.wait_ge(n_st, call)
                for t in range(TILES):
                    last = v.bn_aggr(mvo[:, t, :], sto[:, t, :])
                last.then_inc(n_ag, 1)
                dve.wait_ge(n_ag, call)
                v.tensor_scalar(rstd[:, :], mvo[:, :, 1], 1e-5, None, ALU.add).then_inc(n_eps, 1)
                dve.wait_ge(n_pow, call)
                for t in range(TILES):
                    last = v.tensor_scalar(dst(t), qk[:, t * P:(t + 1) * P], mvo[:, t, 0:1], rstd[:, t:t + 1],
                                           ALU.subtract, ALU.mult)
                    if sm is v_z:
                        last.then_inc(v_z, 1)
                    elif t % POS == POS - 1:
                        last.then_inc(sm, 1)

            def zslot(t):
                return Z[:, (t + t // POS + 1) * P:(t + t // POS + 2) * P]

            def step(k):
                if k.on(L_S) and k.parity(L_S) == 0:
                    k.wait(a_kT, L_S + 1)
                    k.wait(p_S, L_S + 1)
                    fl = k.off("flag", L_S, lambda u: u % TILES)
                    v.tensor_scalar(kT[:, :, 0:WIN], kT[:, :, 2 * P:2 * P + WIN], kflag[:, bass.ds(fl, 1)], None,
                                    ALU.mult).then_inc(v_car, 1)
                if k.on(L_AV):
                    k.wait(p_S, L_AV)
                    s4 = sps[:, :, :].rearrange("p t (a j) -> p t a j", j=2 * WIN)
                    v.tensor_reduce(mx[:, :], s4, AX, ALU.max).then_inc(v_mx, 1)
                    k.wait(v_mx, L_AV)
                    k.wait(p_pT, L_AV + 1)
                    v.tensor_tensor(prob[:, :, :, :].rearrange("p a t j -> p t a j"), s4,
                                    mx[:, :].rearrange("p (t a) -> p t a", t=2).unsqueeze(3)
                                    .to_broadcast([P, 2, PAIRS, 2 * WIN]), ALU.subtract).then_inc(v_sub, 1)
                if k.on(L_WO):
                    k.wait(p_wo, L_WO)
                    k.wait_pair(d_xs, L_WO - 1, 64)
                    zs = Z[:, bass.ds(k.slot(L_WO), P)]
                    v.tensor_tensor(zs, zs, ops[:, 0, 0:P], ALU.add).then_inc(v_z1, 1)
                if k.on(L_F2):
                    if k.reg is None:
                        k.wait(v_z, L_F2 + 1, base=(k.h + 1) * TILES)
                    k.wait(p_f2, L_F2)
                    at = k.layer(L_F2, P)
                    v.tensor_tensor(z2t[:, :], ops[:, 1, 3 * P:4 * P], b2[:, bass.ds(at, P)], ALU.add).then_inc(v_z2a, 1)
                if k.on(L_QKV):
                    k.wait(a_sq[1], L_QKV)
                    k.wait(v_rs, L_QKV + 1, per=RS_STEPS)
                    v.tensor_reduce(ssq[:, 0:HEADS], heads(sq[:, :]), AX, ALU.add).then_inc(v_red[0], 1)
                if k.on(L_F2):
                    k.wait(v_z2a, L_F2)
                    k.wait(d_xs2, L_F2 - 1, per=64)
                    zs = Z[:, bass.ds(k.slot(L_F2), P)]
                    v.tensor_tensor(zs, zs, z2t[:, :], ALU.add).then_inc(v_z, 1)
                if k.on(L_AV):
                    k.wait(a_exp, L_AV)
                    v.tensor_reduce(rs[:, :], prob[:, :, :, :].rearrange("p a t j -> p (a t) j"), AX,
                                    ALU.add).then_inc(v_sum, 1)
                    k.wait(v_sum, L_AV)
                    k.wait(g_nrm, L_AV + 1)
                    v.reciprocal(rr[:, :], rs[:, :]).then_inc(v_rec, 1)
                if k.on(L_S):
                    k.wait(p_qT, L_S)
                    k.wait(p_S, L_S + 1)
                    v.tensor_copy(qTz[64:128, :, :, 1, :],
                                  tps[64:128, :, :].rearrange("p a (w i) -> p a w i", i=WIN)).then_inc(v_qT, 1)
                if k.on(L_WO):
                    k.wait(d_xs2, L_WO, per=64)
                    v.bn_stats(st[:, :], xs2[:, :]).then_inc(v_bn, 1)
                if k.on(L_QKV):
                    k.wait(v_bn, L_WO)
                    k.wait(a_sq[3], L_QKV)
                    v.tensor_reduce(ssq[:, HEADS:2 * HEADS], heads(sq[:, :]), AX, ALU.add).then_inc(v_red[1], 1)
                if k.on(L_WO):
                    if not k.on(L_QKV):
                        k.wait(v_bn, L_WO)
                    v.bn_aggr(mv[:, :], st[:, :]).then_inc(v_mv, 1)
                if k.on(L_QKV):
                    base = {"n": 0}

                    def chain(ins):
                        ins.then_inc(v_rs, 1)
                        base["n"] += 1
                        k.wait_within(v_rs, L_QKV, RS_STEPS, base["n"])

                    def newton():
                        chain(v.tensor_tensor(rt[:, :], rn[:, :], rn[:, :], ALU.mult))
                        chain(v.scalar_tensor_tensor(out=rt[:, :], in0=rt[:, :], scalar=-0.5, in1=ssq[:, :],
                                                     op0=ALU.mult, op1=ALU.mult))
                        chain(v.scalar_tensor_tensor(out=rn[:, :], in0=rt[:, :], scalar=1.5, in1=rn[:, :],
                                                     op0=ALU.add, op1=ALU.mult))

                    k.wait(v_red[0], L_QKV)
                    k.wait(v_red[1], L_QKV)
                    k.wait(v_A[1], L_QKV + 1)
                    chain(v.tensor_scalar(ssq[:, :], ssq[:, :], NORM_EPS2, None, ALU.max))
                    chain(v.tensor_scalar(rt[:, :].bitcast(I32), ssq[:, :].bitcast(I32), 1, None,
                                          ALU.logical_shift_right))
                    chain(v.tensor_scalar(rn[:, :].bitcast(I32), rt[:, :].bitcast(I32), -1.0, float(0x5F3759DF),
                                          ALU.mult, ALU.add))
                    newton()
                if k.on(L_WO):
                    k.wait(v_mv, L_WO)
                    v.tensor_scalar(rt2[:, 0:1], mv[:, 1:2], 1e-5, None, ALU.add).then_inc(v_ve, 1)
                if k.on(L_QKV):
                    newton()
                if k.on(L_F):
                    at = k.layer(L_F, 2 * FH)
                    k.wait(p_f[0], L_F)
                    v.tensor_tensor(fa[:, :], proj[:, 0, 0:FH], bp[:, bass.ds(at, FH)], ALU.add).then_inc(v_fa, 1)
                    k.wait(p_f[1], L_F)
                    v.tensor_tensor(fg[:, :], proj[:, 1, 0:FH], bp[:, bass.ds(at + FH, FH)], ALU.add).then_inc(v_fg, 1)
                if k.on(L_QKV):
                    newton()
                    po = k.off("pos", L_QKV, lambda u: (u % POS) * DH + ((u // TILES) % 2) * (4 * POS * DH))
                    k.wait(v_rs, L_QKV, per=RS_STEPS)
                    k.wait(g_tab, L_QKV, base=TILES - 1)
                    for g in range(2):
                        src = heads(qk[:, g * INNER:(g + 1) * INNER])
                        v.tensor_tensor(src, src, rn[:, g * HEADS:(g + 1) * HEADS].unsqueeze(2)
                                        .to_broadcast([P, HEADS, DH]), ALU.mult).then_inc(v_t[g], 1)
                        if g == 0 and k.on(L_WO):
                            k.wait(g_rstd, L_WO)
                            k.wait(p_xnT, L_WO + 1)
                            v.tensor_scalar(xn[:, :], xs2[:, :], mv[:, 0:1], rt2[:, 1:2], ALU.subtract,
                                            ALU.mult).then_inc(v_xn, 1)
                        k.wait(v_t[g], L_QKV)
                        k.wait((p_qT, p_kT)[g], L_QKV + 1)
                        v.tensor_tensor(heads(rot[:, g * INNER:(g + 1) * INNER]), src,
                                        tab[:, bass.ds(po + 2 * g * POS * DH, DH)].unsqueeze(1)
                                        .to_broadcast([P, HEADS, DH]), ALU.mult).then_inc(v_A[g], 1)
                elif k.on(L_WO):
                    k.wait(g_rstd, L_WO)
                    k.wait(p_xnT, L_WO + 1)
                    v.tensor_scalar(xn[:, :], xs2[:, :], mv[:, 0:1], rt2[:, 1:2], ALU.subtract,
                                    ALU.mult).then_inc(v_xn, 1)
                if k.on(L_F):
                    k.wait(a_gelu, L_F)
                    k.wait(p_hT, L_F + 1)
                    v.tensor_tensor(hh[:, 0:FH], fa[:, :], fg[:, :], ALU.mult).then_inc(v_fm, 1)

            v.memset(w2[:, :], 0.0).then_inc(c_zero, 1)
            for ap in (Z[:, 0:P], Z[:, (POS + 1) * P:(POS + 2) * P], qTz[:, :, :, :, :], pTz[:, :, :, :, :], hh[:, :],
                       kT[:, :, :], va[:, :, :], rt2[:, :]):
                v.memset(ap, 0.0)
            v.memset(half[:, :], -0.5)
            v.memset(kflag[:, :], 1.0).then_inc(c_kf, 1)
            dve.wait_ge(c_kf, 1)
            v.memset(kflag[:, 0:1], 0.0)
            v.memset(kflag[:, POS:POS + 1], 0.0).then_inc(c_zero, 1)
            dve.wait_ge(d_x, 16)
            dve.wait_ge(c_zero, 2)
            outer_norm(1, zslot, v_z)
            dve.wait_ge(d_const, CONSTS)
            for n in range(DEPTH):
                last = v.tensor_copy(rot[:, n * P:(n + 1) * P], lnT[:, 1, n:n + 1].to_broadcast([P, P]))
            last.then_inc(c_lnb, 1)
            for n in range(DEPTH):
                dve.wait_ge(c_bps, n + 1)
                for c in range(2):
                    at = bp[:, (2 * n + c) * FH:(2 * n + c + 1) * FH]
                    last = v.tensor_tensor(at, at, proj[:, c, 0:FH], ALU.add)
                last.then_inc(c_bp, 1)
                at = w1[:, 2 * n * FH:2 * (n + 1) * FH]
                v.tensor_scalar(at, at, lnT[:, 0, n:n + 1], None, ALU.mult).then_inc(c_w1, 1)
            dve.wait_ge(c_bp, DEPTH)
            pipeline(dve, 0, step)

            dve.wait_ge(d_x, 32)
            dve.wait_ge(v_z, TILES + N)
            for b in range(BATCH):
                s0 = (b * (POS + 1) + 1) * P
                part = qk[:, b * INNER:(b + 1) * INNER]
                last = v.scalar_tensor_tensor(out=part, in0=Z[:, s0:s0 + POS * P], scalar=0.5, in1=part,
                                              op0=ALU.mult, op1=ALU.add)
            last.then_inc(n_x1, 1)
            dve.wait_ge(n_x1, 1)
            dve.wait_ge(p_kT, N)
            outer_norm(2, lambda t: rot[:, t * P:(t + 1) * P], n_xn)
            dve.wait_ge(g_add[1], N)
            dve.wait_ge(p_wo, N)
            dve.wait_ge(c_sig, 1)
            for b in range(BATCH):
                part = qk[:, b * INNER:(b + 1) * INNER]
                dve.wait_ge(r_h, b + 1)
                v.tensor_scalar(swp[:, :], proj[:, :, :].rearrange("p a b -> p (a b)"), cols[:, 0:1], cols[:, 2:3],
                                ALU.add, ALU.mult).then_inc(r_bh, 1)
                dve.wait_ge(r_bh, b + 1)
                if b:
                    dve.wait_ge(r_o, b)
                v.tensor_tensor_scan(oT[:, :, :].rearrange("p a b -> p (a b)"), cols[:, 3:4].to_broadcast([P, SEQ]), swp[:, :], 0.0,
                                     ALU.mult, ALU.add).then_inc(r_y, 1)
                dve.wait_ge(r_o, b + 1)
                v.tensor_tensor(part, part, sps[:, :, :].rearrange("p a b -> p (a b)"), ALU.add).then_inc(r_x2a, 1)
                dve.wait_ge(r_x2a, b + 1)
                v.tensor_tensor(tiles3(part), tiles3(part), boB[:, :].unsqueeze(1).to_broadcast([P, POS, P]),
                                ALU.add).then_inc(r_x2, 1)
            dve.wait_ge(r_x2, BATCH)
            outer_norm(3, zslot, v_z)
            pipeline(dve, 1, step)
            dve.wait_ge(d_x, 48)
            dve.wait_ge(v_z, 2 * (TILES + N))
            dve.wait_ge(p_kT, 2 * N)
            for b in range(BATCH):
                s0 = (b * (POS + 1) + 1) * P
                last = v.scalar_tensor_tensor(out=rot[:, b * INNER:(b + 1) * INNER], in0=Z[:, s0:s0 + POS * P],
                                              scalar=0.5, in1=qk[:, b * INNER:(b + 1) * INNER], op0=ALU.mult,
                                              op1=ALU.add)
            last.then_inc(f_out, 1)

        @block.gpsimd
        def _(pool):
            g_ = nc.gpsimd

            def tables(k, src, dst, scale):
                g_.tensor_tensor(tab[:, bass.ds(dst, 2 * DH)].rearrange("p (a d) -> p a d", d=DH),
                                 rope[:, bass.ds(src, 2 * DH)].rearrange("p (a d) -> p a d", d=DH),
                                 scl2[:, bass.ds(scale, DH)].unsqueeze(1).to_broadcast([P, 2, DH]),
                                 ALU.mult).then_inc(g_tab, 1)

            scl2 = scl[:, :, :, :].rearrange("p l k d -> p (l k d)")

            def step(k):
                if k.on(L_AV):
                    k.wait(v_rec, L_AV)
                    pr = prob[:, :, :, :].rearrange("p a t j -> p (a t) j")
                    g_.tensor_tensor(pr, pr, rr[:, :].unsqueeze(2).to_broadcast([P, HEADS, 2 * WIN]),
                                     ALU.mult).then_inc(g_nrm, 1)
                if k.on(L_WO):
                    k.wait(v_ve, L_WO)
                    k.wait(v_xn, L_WO + 1)
                    g_.tensor_tensor(rt2[:, 1:2], rt2[:, 0:1], half[:, 0:1], ALU.pow).then_inc(g_rstd, 1)
                if k.on(L_QKV):
                    po = k.off("pos", L_QKV, lambda u: (u % POS) * DH + ((u // TILES) % 2) * (4 * POS * DH))
                    hd = DH // 2
                    for g in range(2):
                        k.wait(v_t[g], L_QKV)
                        if g == 0:
                            k.wait(g_add[1], L_QKV + 1)
                        else:
                            k.wait(g_add[0], L_QKV)
                        src = qk[:, g * INNER:(g + 1) * INNER]
                        swapped = bass.AP(src.tensor, src.offset + hd,
                                          [list(src.ap[0]), [DH, HEADS], [-hd, 2], [1, hd]])
                        t = tab[:, bass.ds(po + (2 * g + 1) * POS * DH, DH)]
                        g_.tensor_tensor(halves(swp[:, :]), swapped,
                                         t.rearrange("p (a d) -> p a d", a=2).unsqueeze(1)
                                         .to_broadcast([P, HEADS, 2, hd]), ALU.mult).then_inc(g_B[g], 1)
                        k.wait(g_B[g], L_QKV)
                        k.wait(v_A[g], L_QKV)
                        r = rot[:, g * INNER:(g + 1) * INNER]
                        g_.tensor_tensor(r, r, swp[:, :], ALU.add).then_inc(g_add[g], 1)
                    src = k.off("rsrc", L_QKV, lambda u: (u % TILES) * (2 * DH))
                    dst = k.off("rdst", L_QKV, lambda u: ((u + TILES) % (2 * TILES)) * (2 * DH))
                    sc = k.off("rscl", L_QKV, lambda u: ((u - k.h * N) // 4) * DH + 4 * DH)
                    tables(k, src, dst, sc)

            def outer_pow(call):
                pool.wait_ge(n_eps, call)
                g_.tensor_tensor(rstd[:, :], rstd[:, :], half[:, :], ALU.pow).then_inc(n_pow, 1)

            pool.wait_ge(c_zero, 2)
            outer_pow(1)
            pool.wait_ge(d_const, CONSTS)
            for t in range(TILES):
                tables(None, t * 2 * DH, t * 2 * DH, (t // 4) * DH)
            pipeline(pool, 0, step)
            outer_pow(2)
            outer_pow(3)
            pipeline(pool, 1, step)


_INS = ["L0_attn_x", "L0_attn_w_in", "L0_attn_b_in", "L0_attn_a", "L0_attn_b", "L0_attn_w_out", "L0_attn_b_out",
        "L0_ffn_Wqkv", "L0_ffn_q_scale", "L0_ffn_k_scale", "L0_ffn_Wo", "L0_ffn_ln_g", "L0_ffn_ln_b",
        "L0_ffn_W1", "L0_ffn_b1", "L0_ffn_W2", "L0_ffn_b2"]


def _constants():
    f = np.float32
    half = np.arange(0, DH, 2, dtype=f)
    inv_freq = (f(1.0) / np.power(f(10000.0), half / f(DH), dtype=f)).astype(f)
    t = np.arange(SEQ, dtype=f)
    freqs = t[:, None] * inv_freq[None, :]
    freqs = np.concatenate([freqs, freqs], -1)
    base = ((half + f(0.4 * DH)) / f(1.4 * DH)).astype(f)
    scale = np.power(base[None, :], ((t - SEQ // 2) / f(WIN // 2))[:, None], dtype=f)
    scale = np.concatenate([scale, scale], -1)
    sign = np.where(np.arange(DH) < DH // 2, f(-1), f(1))
    cos, sin = np.cos(freqs), np.sin(freqs) * sign
    kinds = np.stack([cos * scale * f(QK_SCALE), sin * scale * f(QK_SCALE), cos / scale, sin / scale])
    rope = kinds.reshape(4, POS, P, DH).transpose(2, 0, 1, 3).reshape(P, 4 * POS * DH).astype(f)
    row = np.arange(P)
    i, g = (row % WIN)[:, None], (row // (2 * WIN))[:, None]
    j = (np.arange(512) % (2 * WIN))[None, :]
    usual = ((j < WIN) & (j >= i)) | ((j >= WIN) & (j - WIN <= i))
    first = np.where(g == 0, usual & (j >= WIN), usual)
    mask = np.concatenate([np.where(m, 0.0, NEG) for m in (usual, first)], 1).astype(f)
    return {"rope": rope, "mask": mask, "ident": np.eye(P, dtype=f)}


def kernel(**inputs):
    import concourse.bacc as _bacc
    from concourse.bass_utils import run_bass_kernel_spmd as _run

    nc = _bacc.Bacc("TRN2", target_bir_lowering=False, num_devices=1)
    arrays, args = {}, []
    for name in _INS:
        a = np.ascontiguousarray(inputs[name])
        arrays[f"in_{name}"] = a
        args.append(nc.dram_tensor(f"in_{name}", a.shape, mybir.dt.from_np(a.dtype), kind="ExternalInput").ap())
    for name, a in _constants().items():
        arrays[f"const_{name}"] = a
        args.append(nc.dram_tensor(f"const_{name}", a.shape, mybir.dt.from_np(a.dtype), kind="ExternalInput").ap())
    x2 = nc.dram_tensor("x2_scratch", (P, TILES * P), F32).ap()
    out = nc.dram_tensor("out_0", (BATCH, SEQ, P), F32, kind="ExternalOutput").ap()
    macaron(nc, *args, x2, out)
    r = _run(nc, [arrays], core_ids=[0])
    return r.results[0]["out_0"]
```

```python
from contextlib import ExitStack

import numpy as np

import concourse.bass as bass
from concourse import mybir

F32 = mybir.dt.float32
BF16 = mybir.dt.bfloat16
I32 = mybir.dt.int32
ALU = mybir.AluOpType
ACT = mybir.ActivationFunctionType
AX = mybir.AxisListType.X

P = 128
DEPTH, HEADS, DH, WIN = 6, 16, 64, 32
BATCH, SEQ = 2, 1024
INNER = HEADS * DH
PAIRS = HEADS // 2
POS = SEQ // P
TILES = BATCH * POS
N = DEPTH * TILES
SLOTS = BATCH * (POS + 1)
FH = P * 4 * 2 // 3
FC = (FH + 2) // 3
QK_SCALE = 8.0
NEG = -1.0e30
NORM_EPS2 = 1e-24

L_X, L_QKV, L_S, L_AV, L_WO, L_F, L_F2 = 0, 1, 2, 3, 4, 5, 6
FRONT = 6
UNROLL = 2


def macaron(nc, x_in, w_in, b_in, a_in, b_gain, w_out, b_out, w_qkv, q_scale, k_scale, w_o,
            ln_g, ln_b, w_1, b_1, w_2, b_2, c_rope, c_mask, c_ident, x2_dram, out):
    with ExitStack() as ctx:
        def sb(name, shape, dt=F32):
            return ctx.enter_context(nc.sbuf_tensor(name, [P] + shape, dt))

        def sem(name):
            return ctx.enter_context(nc.semaphore(name))

        Z = sb("Z", [SLOTS * P])
        qk = sb("qk", [2 * INNER])
        rot = sb("rot", [2 * INNER])
        swp = sb("swp", [INNER])
        sq = sb("sq", [2 * INNER])
        kT = sb("kT", [PAIRS, WIN + 2 * P])
        qTz = sb("qTz", [PAIRS, 4, 2, WIN])
        prob = sb("prob", [PAIRS, 2, 2 * WIN])
        pTz = sb("pTz", [PAIRS, 4, 2, WIN])
        oT = sb("oT", [PAIRS, P])
        va = sb("va", [2, INNER])
        vb = sb("vb", [INNER])
        wq = sb("wq", [2, 3 * INNER])
        wo = sb("wo", [2 * PAIRS * P])
        tab = sb("tab", [2 * 4 * POS * DH])
        rope = sb("rope", [4 * POS * DH])
        scl = sb("scl", [DEPTH + 1, 4, DH])
        w1 = sb("w1", [DEPTH * 2 * FH])
        w2 = sb("w2", [DEPTH * 3 * P])
        bp = sb("bp", [DEPTH * 2 * FH])
        b2 = sb("b2", [DEPTH * P])
        mask = sb("mask", [2 * 512], BF16)
        idf = sb("idf", [P])
        idb = sb("idb", [P], BF16)
        xs = sb("xs", [2, P])
        xsT = sb("xsT", [2, P])
        xs2 = sb("xs2", [P])
        xn = sb("xn", [P])
        xnT = sb("xnT", [P])
        fa = sb("fa", [FH])
        fg = sb("fg", [FH])
        hh = sb("hh", [3 * FC])
        hT = sb("hT", [3, P])
        z2t = sb("z2t", [P])
        ssq = sb("ssq", [2 * HEADS])
        rn = sb("rn", [2 * HEADS])
        rt = sb("rt", [2 * HEADS])
        mx = sb("mx", [HEADS])
        rs = sb("rs", [HEADS])
        rr = sb("rr", [HEADS])
        st = sb("st", [6])
        sto = sb("sto", [TILES, 6])
        mv = sb("mv", [2])
        rt2 = sb("rt2", [4])
        mvo = sb("mvo", [TILES, 2])
        rstd = sb("rstd", [TILES])
        half = sb("half", [TILES])
        kflag = sb("kflag", [TILES])
        cols = sb("cols", [8])
        lnT = sb("lnT", [2, DEPTH])
        winT = sb("winT", [P])
        woutT = sb("woutT", [P])
        boB = sb("boB", [P])

        proj = ctx.enter_context(nc.psum_tensor("proj", [P, 2, 512], F32))
        sps = ctx.enter_context(nc.psum_tensor("sps", [P, 2, 512], F32))
        tps = ctx.enter_context(nc.psum_tensor("tps", [P, PAIRS, P], F32))
        ops = ctx.enter_context(nc.psum_tensor("ops", [P, 2, 512], F32))

        d_id = sem("d_id")
        d_mlp, d_late = sem("d_mlp"), sem("d_late")
        d_const = sem("d_const")
        d_wq, d_wo = sem("d_wq"), sem("d_wo")
        d_xs = [sem(f"d_xs{g}") for g in range(2)]
        d_xs2 = sem("d_xs2")
        d_vb = sem("d_vb")
        d_x = sem("d_x")
        d_out = sem("d_out")
        c_zero, c_zero2 = sem("c_zero"), sem("c_zero2")
        s_idb, s_mask = sem("s_idb"), sem("s_mask")
        c_lnb = sem("c_lnb")
        c_bps, c_bp, c_w1 = sem("c_bps"), sem("c_bp"), sem("c_w1")
        c_wTp, c_wT = sem("c_wTp"), sem("c_wT")
        c_kf, c_scl = sem("c_kf"), sem("c_scl")
        c_sig = sem("c_sig")
        n_st, n_ag, n_eps, n_pow = sem("n_st"), sem("n_ag"), sem("n_eps"), sem("n_pow")
        n_x1, n_xn = sem("n_x1"), sem("n_xn")
        r_xTp, r_xT, r_h, r_bo, r_bh, r_y, r_o, r_x2 = [sem(n) for n in (
            "r_xTp", "r_xT", "r_h", "r_bo", "r_bh", "r_y", "r_o", "r_x2")]
        f_out = sem("f_out")
        p_xT, p_qT, p_kT, p_S, p_pT = sem("p_xT"), sem("p_qT"), sem("p_kT"), sem("p_S"), sem("p_pT")
        p_qkv = [sem(f"p_qkv{c}") for c in range(4)]
        p_v = [sem(f"p_v{c}") for c in range(2)]
        p_f = [sem(f"p_f{c}") for c in range(2)]
        p_O, p_wo, p_xnT, p_hT, p_f2 = [sem(n) for n in ("p_O", "p_wo", "p_xnT", "p_hT", "p_f2")]
        a_xT, a_qT, a_kT, a_pT, a_oT = [sem(n) for n in ("a_xT", "a_qT", "a_kT", "a_pT", "a_oT")]
        a_cp = [sem(f"a_cp{c}") for c in range(4)]
        a_sq = [sem(f"a_sq{c}") for c in range(4)]
        a_v = [sem(f"a_v{c}") for c in range(2)]
        a_exp, a_xnT, a_hT, a_gelu = [sem(n) for n in ("a_exp", "a_xnT", "a_hT", "a_gelu")]
        v_qT, v_car, v_bn, v_mv, v_ve, v_xn = [sem(n) for n in ("v_qT", "v_car", "v_bn", "v_mv", "v_ve", "v_xn")]
        v_t, v_A, v_red = [[sem(f"{n}{g}") for g in range(2)] for n in ("v_t", "v_A", "v_red")]
        v_rs = sem("v_rs")
        v_mx, v_sub, v_sum, v_rec = [sem(n) for n in ("v_mx", "v_sub", "v_sum", "v_rec")]
        v_z1, v_fa, v_fg, v_fm, v_z2a, v_z = [sem(n) for n in ("v_z1", "v_fa", "v_fg", "v_fm", "v_z2a", "v_z")]
        g_B, g_add = [[sem(f"{n}{g}") for g in range(2)] for n in ("g_B", "g_add")]
        g_tab, g_rstd, g_nrm = sem("g_tab"), sem("g_rstd"), sem("g_nrm")
        RS_STEPS = 11

        block = ctx.enter_context(nc.Block())

        class Step:

            def __init__(self, eng, h, reg, s, memo):
                self.eng, self.h, self.reg, self.s, self.memo = eng, h, reg, s, memo

            def on(self, lag):
                return self.reg is not None or 0 <= self.s - lag < N

            def val(self, key, f):
                if key not in self.memo:
                    self.memo[key] = self.eng.snap(f())
                return self.memo[key]

            def tile(self, lag):
                if self.reg is None:
                    return self.h * N + self.s - lag
                return self.reg + (self.s - lag)

            def parity(self, lag):
                return (self.s - lag) % 2

            def wait(self, sm, lag, per=1, base=0):
                if self.reg is None:
                    u = min(self.s - lag, N - 1)
                    if u < 0:
                        return
                    self.eng.wait_ge(sm, (self.h * N + u + 1) * per + base)
                elif per == 1:
                    self.eng.wait_ge(sm, self.count(lag, base))
                else:
                    c = (self.s - lag + 1) * per + base
                    self.eng.wait_ge(sm, self.val(("w", per, c), lambda: self.reg * per + c))

            def count(self, lag, base=0):
                c = self.s - lag + 1 + base
                return self.val(("w", c), lambda: self.reg + c)

            def wait_pair(self, sms, lag, per):
                if self.reg is None:
                    u = min(self.s - lag, N - 1)
                    if u >= 0:
                        self.eng.wait_ge(sms[u % 2], ((self.h * N + u) // 2 + 1) * per)
                else:
                    c = (self.s - lag) // 2 * per + per
                    self.eng.wait_ge(sms[(self.s - lag) % 2],
                                     self.val(("w", per // 2, c), lambda: self.reg * (per // 2) + c))

            def wait_even(self, sm, lag):
                if self.reg is None:
                    u = self.s - lag
                    if u >= 0:
                        self.eng.wait_ge(sm, (self.h * N + u) // 2 + 1)
                else:
                    c = (self.s - lag) // 2 + 1
                    self.eng.wait_ge(sm, self.val(("even", c), lambda: self.reg // 2 + c))

            def wait_within(self, sm, lag, per, n):
                c = (self.s - lag) * per + n
                if self.reg is None:
                    self.eng.wait_ge(sm, self.h * N * per + c)
                else:
                    self.eng.wait_ge(sm, self.val(("w", per, c), lambda: self.reg * per + c))

            def off(self, name, lag, f):
                if self.reg is None:
                    return f(self.tile(lag))
                return self.val((name, self.s - lag), lambda: f(self.tile(lag)))

            def slot(self, lag, back=0, part=0):
                return self.off(("slot", back, part), lag,
                                lambda u: (u % TILES + (u // POS) % 2 + 1 - back) * P + part)

            def layer(self, lag, width):
                if self.reg is None:
                    return ((self.s - lag) // TILES) * width
                return self.off(("layer", width), lag, lambda u: ((u - self.h * N) // TILES) * width)

            def layer_parity(self, lag, width):
                return self.off(("lp", width), lag, lambda u: ((u // TILES) % 2) * width)

        def pipeline(eng, h, step, prepare=None):
            first = h * N
            for s in range(FRONT):
                step(Step(eng, h, None, s, {}))
                if h == 0 and s == MLP_STEP and prepare is not None:
                    prepare()
            with eng.Fori(first + FRONT, first + N, UNROLL) as i:
                memo = {}
                for j in range(UNROLL):
                    step(Step(eng, h, i, j, memo))
            for s in range(N, N + L_F2):
                step(Step(eng, h, None, s, {}))

        def heads(ap):
            return ap.rearrange("p (h d) -> p h d", d=DH)

        def halves(ap):
            return ap.rearrange("p (h a d) -> p h a d", a=2, d=DH // 2)


        def tiles3(ap):
            return ap.rearrange("p (t d) -> p t d", d=P)

        CHUNKS = PAIRS
        WQ = 3 * INNER // CHUNKS
        Q_CHUNKS = -(-2 * INNER // WQ)
        FIRST_Q, FIRST_O = CHUNKS - Q_CHUNKS + 1, 1
        W_Q, W_O = L_S, L_WO
        mlp_consts = [
            (lnT[:, 1, :], ln_b.rearrange("l p -> p l")),
            (lnT[:, 0, :], ln_g.rearrange("l p -> p l")),
            (w1[:, :].rearrange("p (l n) -> p l n", l=DEPTH), w_1.rearrange("l p n -> p l n")),
        ]
        consts = [(rope[:, :], c_rope)]
        for kind, src in ((0, q_scale), (2, k_scale)):
            consts.append((scl[:, 0:DEPTH, kind, :], src.partition_broadcast(P)))
        consts += [
            (prob[:, :, :, :].rearrange("p a b c -> p (a b c)"), c_mask),
            (boB[:, :], b_out.partition_broadcast(P)),
            (winT[:, :], w_in), (woutT[:, :], w_out),
            (cols[:, 0:1], b_in.rearrange("(p a) -> p a", a=1)),
            (cols[:, 1:2], a_in.rearrange("(p a) -> p a", a=1)),
            (cols[:, 2:3], b_gain.rearrange("(p a) -> p a", a=1)),
        ]
        late_consts = [
            (bp[:, :].rearrange("p (l n) -> p l n", l=DEPTH), b_1.partition_broadcast(P)),
            (b2[:, :].rearrange("p (l n) -> p l n", l=DEPTH), b_2.partition_broadcast(P)),
        ]
        w2v = w2[:, :].rearrange("p (l c n) -> p l c n", l=DEPTH, c=3)
        for c in range(3):
            rows = min(FC, FH - c * FC)
            late_consts.append((w2v[0:rows, :, c, :], w_2[:, c * FC:c * FC + rows, :].rearrange("l p n -> p l n")))
        MLP_STEP = 1
        pairs = [sps, ops]

        @block.sync
        def _(sp):
            def load_q(layer, at_q, at):
                sp.dma_start(wq[:, :, :].rearrange("p a n -> p (a n)")[:, at_q],
                             w_qkv[layer].rearrange("a p n -> p (a n)")[:, at]).then_inc(d_wq, 16)

            def load_o(layer, at_o, rows):
                sp.dma_start(wo[:, at_o], w_o[layer].rearrange("a p n -> (a p) n")[rows]).then_inc(d_wo, 16)

            def load_weights(k):
                if k.reg is None:
                    for first, load, sm in ((W_Q, load_q, d_wq), (W_O, load_o, d_wo)):
                        m = k.s - first
                        if m < 0 or m % 2 or k.s >= (N + first if k.h == 0 else N):
                            continue
                        layer, c = m // TILES + 1, m % TILES // 2
                        few = FIRST_Q if load is load_q else FIRST_O
                        sp.wait_ge(sm, 16 * (CHUNKS * k.h * DEPTH + (layer - 1) * CHUNKS + few + c))
                        p = (k.h * DEPTH + layer) % 2
                        w = layer % DEPTH
                        if load is load_q:
                            load(slice(w, w + 1), slice(p * 3 * INNER + c * WQ, p * 3 * INNER + (c + 1) * WQ),
                                 slice(c * WQ, (c + 1) * WQ))
                        else:
                            load(slice(w, w + 1), slice((p * PAIRS + c) * P, (p * PAIRS + c + 1) * P),
                                 slice(c * P, (c + 1) * P))
                elif k.s == 0:
                    for first, load, sm in ((W_Q, load_q, d_wq), (W_O, load_o, d_wo)):
                        u = k.reg - first
                        w = k.val(("w_layer", first), lambda: ((u - k.h * N) // TILES + 1) % DEPTH)
                        c = k.val(("w_chunk", first), lambda: (u % TILES) // 2)
                        p = k.val(("w_parity", first), lambda: (u // TILES + 1) % 2)
                        few = FIRST_Q if load is load_q else FIRST_O
                        done = k.val(("w_done", first), lambda: (u // 2 + few) * 16)
                        if load is load_q:
                            to = k.val("q_to", lambda: p * (3 * INNER) + c * WQ)
                            at = k.val("q_at", lambda: c * WQ)
                            sp.wait_ge(sm, done)
                            load(bass.ds(w, 1), bass.ds(to, WQ), bass.ds(at, WQ))
                        else:
                            to = k.val("o_to", lambda: p * (PAIRS * P) + c * P)
                            at = k.val("o_at", lambda: c * P)
                            sp.wait_ge(sm, done)
                            load(bass.ds(w, 1), bass.ds(to, P), bass.ds(at, P))

            def shift(k, lag, dst, sm):
                hf, cut = P // 2, P - 16
                new, tail, left = k.slot(lag), k.slot(lag, 0, hf), k.slot(lag, 1, hf)
                sp.dma_start(dst[:, 0:hf], Z[:, bass.ds(new, hf)]).then_inc(sm, 16)
                sp.dma_start(dst[1:cut + 1, hf:P], Z[0:cut, bass.ds(tail, hf)]).then_inc(sm, 16)
                sp.dma_start(dst[cut + 1:P, hf:P], Z[cut:P - 1, bass.ds(tail, hf)]).then_inc(sm, 16)
                sp.dma_start(dst[0:1, hf:P], Z[P - 1:P, bass.ds(left, hf)]).then_inc(sm, 16)

            sp.dma_start(tiles3(qk[:, :]), x_in.rearrange("b (t p) d -> p (b t) d", p=P)).then_inc(d_x, 16)
            sp.dma_start(idf[:, :], c_ident).then_inc(d_id, 16)
            load_q(slice(0, 1), slice(0, 2 * INNER), slice(0, 2 * INNER))

            def first_weights():
                sp.wait_ge(d_wq, 16)
                for c in range(FIRST_Q - 1):
                    w = INNER // (FIRST_Q - 1)
                    at = slice(2 * INNER + c * w, 2 * INNER + (c + 1) * w)
                    load_q(slice(0, 1), at, at)
                sp.dma_start(wo[:, 0:PAIRS * P].rearrange("p (c n) -> p c n", n=P),
                             w_o[0].rearrange("(c p) n -> p c n", p=P)).then_inc(d_wo, 16)
                for dst, src in mlp_consts:
                    sp.dma_start(dst, src, allow_slow_non_contiguous=True).then_inc(d_mlp, 16)

            def step(k):
                if k.reg is not None:
                    for lag in (L_X, L_WO):
                        k.slot(lag), k.slot(lag, 0, P // 2), k.slot(lag, 1, P // 2)
                if k.on(L_WO):
                    k.wait(v_z1, L_WO)
                    shift(k, L_WO, xs2[:, :], d_xs2)
                if k.on(L_X):
                    k.wait(v_z, L_X, base=k.h * TILES)
                    if k.reg is None:
                        k.wait(p_xT, L_X + 2)
                    shift(k, L_X, xs[:, k.parity(L_X), :], d_xs[k.parity(L_X)])
                if k.on(L_S):
                    if k.reg is None:
                        k.wait(a_v[1], L_S)
                    k.wait(a_oT, L_AV)
                    par = k.parity(L_S)
                    sp.dma_start(vb[WIN:P, :], va[0:P - WIN, par, :]).then_inc(d_vb, 16)
                    sp.dma_start(vb[0:WIN, :], va[P - WIN:P, 1 - par, :]).then_inc(d_vb, 16)
                if k.h == 0 and k.reg is None and k.s == 0:
                    first_weights()
                load_weights(k)

            sp.wait_ge(c_zero2, 1)
            pipeline(sp, 0, step)
            sp.wait_ge(v_A[1], N)
            sp.wait_ge(g_B[1], N)
            sp.dma_start(tiles3(qk[:, :]), x_in.rearrange("b (t p) d -> p (b t) d", p=P)).then_inc(d_x, 16)
            sp.wait_ge(r_x2, BATCH)
            sp.dma_start(x2_dram, qk[:, :]).then_inc(d_out, 16)
            pipeline(sp, 1, step)
            sp.wait_ge(v_A[1], 2 * N)
            sp.wait_ge(g_B[1], 2 * N)
            sp.dma_start(qk[:, :], x2_dram).then_inc(d_x, 16)
            for b in range(BATCH):
                sp.wait_ge(f_out, b + 1)
                sp.dma_start(out[b].rearrange("(t p) d -> p t d", p=P),
                             tiles3(rot[:, b * INNER:(b + 1) * INNER])).then_inc(d_out, 16)
            sp.wait_ge(d_out, 16 * (1 + BATCH))
            sp.wait_ge(d_wq, 16 * (CHUNKS * 2 * DEPTH + FIRST_Q - W_Q // 2))
            sp.wait_ge(d_wo, 16 * (CHUNKS * 2 * DEPTH + FIRST_O - W_O // 2))

        @block.tensor
        def _(pe):
            mm, tr = nc.tensor.matmul, nc.tensor.transpose

            def qkv(k, c):
                w = k.layer_parity(L_QKV, 3 * INNER)
                mm(proj[:, c % 2, :], xsT[:, k.parity(L_QKV), :],
                   wq2[:, bass.ds(w + c * 512, 512)], start=True, stop=True).then_inc(p_qkv[c], 1)

            def weights(k, lag, sm, chunks):
                n = chunks - CHUNKS + (FIRST_Q if sm is d_wq else FIRST_O)
                if k.reg is None:
                    pe.wait_ge(sm, ((k.tile(lag) // TILES) * CHUNKS + n) * 16)
                else:
                    pe.wait_ge(sm, k.off(("weights", n), lag, lambda u: ((u // TILES) * CHUNKS + n) * 16))

            wq2 = wq[:, :, :].rearrange("p a n -> p (a n)")

            def step(k):
                if k.on(L_QKV):
                    weights(k, L_QKV, d_wq, Q_CHUNKS)
                    k.wait(a_xT, L_QKV)
                    for c in range(2):
                        k.wait((v_fa, v_fg)[c], L_F + 1)
                        if k.reg is None:
                            k.wait(a_v[c], L_S + 1)
                        qkv(k, c)
                if k.on(L_F2):
                    k.wait(v_fm, L_F2)
                    k.wait(a_oT, L_AV + 1)
                    for c in range(3):
                        last = tr(ops[0:FC, 1, c * P:(c + 1) * P], hh[:, c * FC:(c + 1) * FC], idf[:, :])
                    last.then_inc(p_hT, 1)
                if k.on(L_F):
                    k.wait(v_xn, L_F)
                    k.wait(a_pT, L_AV + 1)
                    tr(tps[:, 0, :], xn[:, :], idf[:, :]).then_inc(p_xnT, 1)
                if k.on(L_WO):
                    weights(k, L_WO, d_wo, CHUNKS)
                    k.wait(a_oT, L_WO)
                    w = k.layer_parity(L_WO, PAIRS * P)
                    for p in range(PAIRS):
                        last = mm(ops[:, 0, 0:P], oT[:, p, :], wo[:, bass.ds(w + p * P, P)], start=(p == 0),
                                  stop=(p == PAIRS - 1))
                    last.then_inc(p_wo, 1)
                if k.on(L_S):
                    k.wait(g_add[0], L_S)
                    k.wait(a_xnT, L_F)
                    for p in range(PAIRS):
                        last = tr(tps[:, p, :], rot[:, p * P:(p + 1) * P], idf[:, :])
                    last.then_inc(p_qT, 1)
                if k.on(L_QKV):
                    k.wait(a_sq[0], L_QKV)
                    qkv(k, 2)
                    k.wait(a_sq[1], L_QKV)
                    qkv(k, 3)
                if k.on(L_F2):
                    k.wait(a_hT, L_F2)
                    at = k.layer(L_F2, 3 * P)
                    for c in range(3):
                        last = mm(ops[:, 1, 3 * P:4 * P], hT[0:FC, c, :], w2[0:FC, bass.ds(at + c * P, P)],
                                  start=(c == 0), stop=(c == 2))
                    last.then_inc(p_f2, 1)
                if k.on(L_S):
                    k.wait(g_add[1], L_S)
                    k.wait(a_qT, L_S)
                    k.wait(v_qT, L_S)
                    for p in range(PAIRS):
                        last = tr(tps[:, p, :], rot[:, INNER + p * P:INNER + (p + 1) * P], idf[:, :])
                    last.then_inc(p_kT, 1)
                if k.on(L_S):
                    weights(k, L_S, d_wq, CHUNKS)
                    w = k.layer_parity(L_S, 3 * INNER)
                    for c in range(2):
                        k.wait(a_sq[2 + c], L_QKV)
                        mm(proj[:, c, :], xsT[:, k.parity(L_S), :], wq2[:, bass.ds(w + (4 + c) * 512, 512)],
                           start=True, stop=True).then_inc(p_v[c], 1)
                if k.on(L_AV):
                    k.wait(g_nrm, L_AV)
                    k.wait(a_kT, L_S)
                    k.wait(a_xnT, L_F)
                    for p in range(PAIRS):
                        last = tr(tps[:, p, :], prob[:, p, :, :].rearrange("p a b -> p (a b)"), idf[:, :])
                    last.then_inc(p_pT, 1)
                if k.on(L_F):
                    k.wait(a_xnT, L_F)
                    at = k.layer(L_F, 2 * FH)
                    for c in range(2):
                        k.wait(a_v[c], L_S)
                        mm(proj[:, c, 0:FH], xnT[:, :], w1[:, bass.ds(at + c * FH, FH)],
                           start=True, stop=True).then_inc(p_f[c], 1)
                if k.on(L_S):
                    k.wait(v_sub, L_S + 1)
                    k.wait(a_qT, L_S)
                    k.wait(v_qT, L_S)
                    k.wait(a_kT, L_S)
                    if k.parity(L_S) == 0:
                        k.wait_even(v_car, L_S)
                    first = k.off("first", L_S, lambda u: ((POS - 1 - u % POS) // (POS - 1)) * 512)
                    par = k.parity(L_S)
                    for ty in range(2):
                        m = mask[:, bass.ds(first, 512)] if ty == 0 else mask[:, 0:512]
                        mm(sps[:, ty, :], idb[:, :], m, start=True, stop=False, skip_group_check=True)
                        for p in range(PAIRS):
                            for g in range(2):
                                w = 2 * ty + g
                                at = par * P + w * WIN
                                last = mm(sps[g * 64:g * 64 + 64, ty, p * 64:p * 64 + 64],
                                          qTz[:, p, w, :, :].rearrange("p a b -> p (a b)"), kT[:, p, at:at + 2 * WIN],
                                          start=False, stop=True, skip_group_check=True)
                    last.then_inc(p_S, 1)
                if k.on(L_X):
                    k.wait_pair(d_xs, L_X, 64)
                    k.wait(a_kT, L_S)
                    k.wait(a_pT, L_AV)
                    tr(tps[:, 4, :], xs[:, k.parity(L_X), :], idf[:, :]).then_inc(p_xT, 1)
                if k.on(L_AV):
                    k.wait(a_pT, L_AV)
                    k.wait(d_vb, L_AV, per=32)
                    k.wait(v_z1, L_WO)
                    k.wait(v_z2a, L_F2)
                    par = k.parity(L_AV)
                    for p in range(PAIRS):
                        o4 = ops[:, p // 4, (p % 4) * P:(p % 4 + 1) * P].rearrange("p (t g i) -> p t g i", t=2, g=2)
                        for g in range(2):
                            for hp in range(2):
                                at = (2 * p + hp) * DH
                                v = vb[:, at:at + DH] if g == 0 else va[:, par, at:at + DH]
                                last = mm(o4[hp * DH:(hp + 1) * DH, :, g, :], v,
                                          pTz[:, p, g * 2 + hp, :, :].rearrange("p a b -> p (a b)"),
                                          start=True, stop=True, skip_group_check=True)
                    last.then_inc(p_O, 1)

            def prepare():
                pe.wait_ge(d_mlp, 16 * len(mlp_consts))
                pe.wait_ge(c_lnb, 1)
                for n in range(DEPTH):
                    if n >= len(pairs):
                        pe.wait_ge(c_bp, n - len(pairs) + 1)
                    for c in range(2):
                        last = mm(pairs[n % len(pairs)][:, c, 0:FH], oT[:, n, :],
                                  w1[:, (2 * n + c) * FH:(2 * n + c + 1) * FH], start=True, stop=True)
                    last.then_inc(c_bps, 1)
                pe.wait_ge(c_bp, DEPTH)
                pe.wait_ge(c_w1, DEPTH)
                pe.wait_ge(d_late, 16 * len(late_consts))
                pe.wait_ge(d_const, 16 * len(consts))
                tr(ops[:, 0, 0:P], winT[:, :], idf[:, :])
                tr(ops[:, 0, P:2 * P], woutT[:, :], idf[:, :]).then_inc(c_wTp, 1)
                pe.wait_ge(c_wT, 1)

            pe.wait_ge(d_id, 16)
            pe.wait_ge(s_idb, 1)
            pe.wait_ge(s_mask, 1)
            pe.wait_ge(c_zero, 2)
            pe.wait_ge(c_zero2, 1)
            pipeline(pe, 0, step, prepare)

            for b in range(BATCH):
                pe.wait_ge(n_xn, b + 1)
                if b:
                    pe.wait_ge(r_xT, b)
                for t in range(POS):
                    last = tr(tps[:, t, :], rot[:, (b * POS + t) * P:(b * POS + t + 1) * P], idf[:, :])
                last.then_inc(r_xTp, 1)
                pe.wait_ge(r_xT, b + 1)
                if b:
                    pe.wait_ge(r_bh, b)
                for c in range(2):
                    at = b * INNER + c * 512
                    last = mm(proj[:, c, :], winT[:, :], sq[:, at:at + 512], start=True, stop=True)
                last.then_inc(r_h, 1)
            for b in range(BATCH):
                pe.wait_ge(r_y, b + 1)
                ys = (oT[:, :, :].rearrange("p a b -> p (a b)"), rot[:, 0:INNER])[b]
                for t in range(POS):
                    last = mm((sps, ops)[b][:, t // 4, (t % 4) * P:(t % 4 + 1) * P], ys[:, t * P:(t + 1) * P],
                              woutT[:, :], start=True, stop=True, skip_group_check=True)
                last.then_inc(r_o, 1)
            pe.wait_ge(r_x2, BATCH)
            pipeline(pe, 1, step)

        @block.scalar
        def _(act):
            fn, cp = nc.scalar.activation, nc.scalar.copy

            def step(k):
                if k.on(L_AV):
                    k.wait(v_sub, L_AV)
                    fn(prob[:, :, :, :], prob[:, :, :, :], ACT.Exp).then_inc(a_exp, 1)
                if k.on(L_F):
                    k.wait(p_xnT, L_F)
                    k.wait(p_f[1], L_F + 1)
                    cp(xnT[:, :], tps[:, 0, :]).then_inc(a_xnT, 1)
                if k.on(L_QKV):
                    k.wait(v_A[0], L_QKV + 1)
                    k.wait(g_B[0], L_QKV + 1)
                    for c in range(2):
                        k.wait(p_qkv[c], L_QKV)
                        cp(qk[:, c * 512:(c + 1) * 512], proj[:, c, :]).then_inc(a_cp[c], 1)
                        if c == 0:
                            k.wait(v_red[0], L_QKV + 1)
                        fn(sq[:, c * 512:(c + 1) * 512], proj[:, c, :], ACT.Square).then_inc(a_sq[c], 1)
                if k.on(L_F2):
                    k.wait(p_hT, L_F2)
                    k.wait(p_f2, L_F2 + 1)
                    cp(hT[0:FC, :, :], ops[0:FC, 1, 0:3 * P].rearrange("p (c n) -> p c n", c=3)).then_inc(a_hT, 1)
                if k.on(L_S):
                    k.wait(p_qT, L_S)
                    k.wait(p_S, L_S + 1)
                    cp(qTz[0:64, :, :, 0, :], tps[0:64, :, :].rearrange("p a (w i) -> p a w i", i=WIN)).then_inc(a_qT, 1)
                if k.on(L_QKV):
                    k.wait(v_A[1], L_QKV + 1)
                    k.wait(g_B[1], L_QKV + 1)
                    k.wait(v_red[1], L_QKV + 1)
                    for c in range(2, 4):
                        k.wait(p_qkv[c], L_QKV)
                        cp(qk[:, c * 512:(c + 1) * 512], proj[:, c - 2, :]).then_inc(a_cp[c], 1)
                        fn(sq[:, c * 512:(c + 1) * 512], proj[:, c - 2, :], ACT.Square).then_inc(a_sq[c], 1)
                if k.on(L_S):
                    k.wait(p_kT, L_S)
                    k.wait(p_S, L_S + 1)
                    if k.parity(L_S) == 1:
                        k.wait_even(v_car, L_S + 1)
                    at = WIN + k.parity(L_S) * P
                    cp(kT[:, :, at:at + P], tps[:, :, :]).then_inc(a_kT, 1)
                if k.on(L_S):
                    k.wait(p_O, L_S + 2)
                    k.wait(d_vb, L_S + 1, per=32)
                    for c in range(2):
                        k.wait(p_v[c], L_S)
                        cp(va[:, k.parity(L_S), c * 512:(c + 1) * 512], proj[:, c, :]).then_inc(a_v[c], 1)
                if k.on(L_AV):
                    k.wait(p_pT, L_AV)
                    k.wait(p_O, L_AV + 1)
                    for t in range(2):
                        rows = slice(t * 64, t * 64 + 64)
                        last = cp(pTz[rows, :, :, t, :], tps[rows, :, :].rearrange("p a (b c) -> p a b c", c=WIN))
                    last.then_inc(a_pT, 1)
                if k.on(L_F):
                    k.wait(v_fg, L_F)
                    fn(fg[:, :], fg[:, :], ACT.Gelu).then_inc(a_gelu, 1)
                if k.on(L_X):
                    k.wait(p_xT, L_X)
                    k.wait(p_v[1], L_X + 2)
                    cp(xsT[:, k.parity(L_X), :], tps[:, 4, :]).then_inc(a_xT, 1)
                if k.on(L_AV):
                    k.wait(p_O, L_AV)
                    k.wait(p_wo, L_AV + 1)
                    cp(oT[:, :, :].rearrange("p a b -> p (a b)"), ops[:, :, :].rearrange("p a b -> p (a b)")).then_inc(a_oT, 1)

            def prepare():
                act.wait_ge(d_mlp, 16 * len(mlp_consts))
                for n in range(DEPTH):
                    act.wait_ge(c_bps, n + 1)
                    at = w1[:, 2 * n * FH:2 * (n + 1) * FH]
                    fn(at, at, ACT.Copy, scale=lnT[:, 0, n:n + 1]).then_inc(c_w1, 1)
                act.wait_ge(c_wTp, 1)
                cp(winT[:, :], ops[:, 0, 0:P])
                cp(woutT[:, :], ops[:, 0, P:2 * P]).then_inc(c_wT, 1)
                fn(cols[:, 3:4], cols[:, 1:2], ACT.Sigmoid).then_inc(c_sig, 1)

            for dst, src in consts:
                act.dma_start(dst, src).then_inc(d_const, 16)
            act.wait_ge(d_id, 16)
            cp(idb[:, :], idf[:, :]).then_inc(s_idb, 1)
            act.wait_ge(d_const, 16 * len(consts))
            cp(mask[:, :], prob[:, :, :, :].rearrange("p a b c -> p (a b c)")).then_inc(s_mask, 1)
            act.wait_ge(v_z, TILES)
            act.wait_ge(c_zero, 2)
            act.wait_ge(c_zero2, 1)
            for dst, src in late_consts:
                act.dma_start(dst, src).then_inc(d_late, 16)
            pipeline(act, 0, step, prepare)
            act.wait_ge(v_red[1], N)
            for b in range(BATCH):
                act.wait_ge(r_xTp, b + 1)
                cp(sq[:, b * INNER:(b + 1) * INNER], tps[:, :, :].rearrange("p a b -> p (a b)")).then_inc(r_xT, 1)
            act.wait_ge(v_z, 2 * TILES + N)
            act.wait_ge(d_out, 16)
            act.wait_ge(r_h, BATCH)
            act.wait_ge(r_o, BATCH)
            pipeline(act, 1, step)

        @block.vector
        def _(dve):
            v = nc.vector

            def norm_stats(call, b):
                rows = range(b * POS, (b + 1) * POS)
                for t in rows:
                    last = v.bn_stats(sto[:, t, :], qk[:, t * P:(t + 1) * P])
                last.then_inc(n_st, 1)
                dve.wait_ge(n_st, call)
                for t in rows:
                    last = v.bn_aggr(mvo[:, t, :], sto[:, t, :])
                last.then_inc(n_ag, 1)
                dve.wait_ge(n_ag, call)
                v.tensor_scalar(rstd[:, b * POS:(b + 1) * POS], mvo[:, b * POS:(b + 1) * POS, 1], 1e-5, None,
                                ALU.add).then_inc(n_eps, 1)

            def norm_apply(call, b, dst, sm):
                dve.wait_ge(n_pow, call)
                for t in range(b * POS, (b + 1) * POS):
                    last = v.tensor_scalar(dst(t), qk[:, t * P:(t + 1) * P], mvo[:, t, 0:1], rstd[:, t:t + 1],
                                           ALU.subtract, ALU.mult)
                    if sm is v_z:
                        last.then_inc(v_z, 1)
                    elif t % POS == POS - 1:
                        last.then_inc(sm, 1)

            def newton(k, n):
                k.wait_within(v_rs, L_QKV, RS_STEPS, n)
                v.tensor_tensor(rt[:, :], rn[:, :], rn[:, :], ALU.mult).then_inc(v_rs, 1)
                k.wait_within(v_rs, L_QKV, RS_STEPS, n + 1)
                v.scalar_tensor_tensor(out=rt[:, :], in0=rt[:, :], scalar=-0.5, in1=ssq[:, :],
                                       op0=ALU.mult, op1=ALU.mult).then_inc(v_rs, 1)
                k.wait_within(v_rs, L_QKV, RS_STEPS, n + 2)
                v.scalar_tensor_tensor(out=rn[:, :], in0=rt[:, :], scalar=1.5, in1=rn[:, :],
                                       op0=ALU.add, op1=ALU.mult).then_inc(v_rs, 1)

            def normalise(k, g):
                src = heads(qk[:, g * INNER:(g + 1) * INNER])
                v.tensor_tensor(src, src, rn[:, g * HEADS:(g + 1) * HEADS].unsqueeze(2)
                                .to_broadcast([P, HEADS, DH]), ALU.mult).then_inc(v_t[g], 1)

            def cosine(k, g):
                po = k.off("pos", L_QKV, lambda u: (u % POS) * DH + ((u // TILES) % 2) * (4 * POS * DH))
                k.wait(v_t[g], L_QKV)
                k.wait((p_qT, p_kT)[g], L_QKV + 1)
                v.tensor_tensor(heads(rot[:, g * INNER:(g + 1) * INNER]), heads(qk[:, g * INNER:(g + 1) * INNER]),
                                tab[:, bass.ds(po + 2 * g * POS * DH, DH)].unsqueeze(1)
                                .to_broadcast([P, HEADS, DH]), ALU.mult).then_inc(v_A[g], 1)

            def zslot(t):
                return Z[:, (t + t // POS + 1) * P:(t + t // POS + 2) * P]

            def step(k):
                if k.on(L_S) and k.parity(L_S) == 0:
                    k.wait(a_kT, L_S + 1)
                    k.wait(p_S, L_S + 1)
                    fl = k.off("flag", L_S, lambda u: u % TILES)
                    v.tensor_scalar(kT[:, :, 0:WIN], kT[:, :, 2 * P:2 * P + WIN], kflag[:, bass.ds(fl, 1)], None,
                                    ALU.mult).then_inc(v_car, 1)
                if k.on(L_AV):
                    k.wait(a_exp, L_AV)
                    v.tensor_reduce(rs[:, :], prob[:, :, :, :].rearrange("p a t j -> p (a t) j"), AX,
                                    ALU.add).then_inc(v_sum, 1)
                if k.on(L_WO):
                    k.wait(p_wo, L_WO)
                    k.wait_pair(d_xs, L_WO - 1, 64)
                    zs = Z[:, bass.ds(k.slot(L_WO), P)]
                    v.tensor_tensor(zs, zs, ops[:, 0, 0:P], ALU.add).then_inc(v_z1, 1)
                if k.on(L_AV):
                    k.wait(v_sum, L_AV)
                    k.wait(g_nrm, L_AV + 1)
                    v.reciprocal(rr[:, :], rs[:, :]).then_inc(v_rec, 1)
                if k.on(L_S):
                    k.wait(p_qT, L_S)
                    k.wait(p_S, L_S + 1)
                    v.tensor_copy(qTz[64:128, :, :, 1, :],
                                  tps[64:128, :, :].rearrange("p a (w i) -> p a w i", i=WIN)).then_inc(v_qT, 1)
                if k.on(L_QKV):
                    k.wait(a_sq[1], L_QKV)
                    k.wait(v_rs, L_QKV + 1, per=RS_STEPS)
                    v.tensor_reduce(ssq[:, 0:HEADS], heads(sq[:, 0:INNER]), AX, ALU.add).then_inc(v_red[0], 1)
                if k.on(L_F2):
                    if k.reg is None:
                        k.wait(v_z, L_F2 + 1, base=(k.h + 1) * TILES)
                    k.wait(p_f2, L_F2)
                    at = k.layer(L_F2, P)
                    v.tensor_tensor(z2t[:, :], ops[:, 1, 3 * P:4 * P], b2[:, bass.ds(at, P)], ALU.add).then_inc(v_z2a, 1)
                if k.on(L_QKV):
                    k.wait(a_sq[3], L_QKV)
                    v.tensor_reduce(ssq[:, HEADS:2 * HEADS], heads(sq[:, INNER:2 * INNER]), AX, ALU.add).then_inc(v_red[1], 1)
                if k.on(L_QKV):
                    k.wait(v_red[0], L_QKV)
                    k.wait(v_red[1], L_QKV)
                    k.wait(v_A[1], L_QKV + 1)
                    v.tensor_scalar(ssq[:, :], ssq[:, :], NORM_EPS2, None, ALU.max).then_inc(v_rs, 1)
                    k.wait_within(v_rs, L_QKV, RS_STEPS, 1)
                    v.tensor_scalar(rn[:, :].bitcast(I32), ssq[:, :].bitcast(I32), -0.5, float(0x5F3759DF),
                                    ALU.mult, ALU.add).then_inc(v_rs, 1)
                    newton(k, 2)
                    newton(k, 5)
                    newton(k, 8)
                if k.on(L_WO):
                    k.wait(d_xs2, L_WO, per=64)
                    v.bn_stats(st[:, :], xs2[:, :]).then_inc(v_bn, 1)
                if k.on(L_F):
                    at = k.layer(L_F, 2 * FH)
                    k.wait(p_f[0], L_F)
                    v.tensor_tensor(fa[:, :], proj[:, 0, 0:FH], bp[:, bass.ds(at, FH)], ALU.add).then_inc(v_fa, 1)
                    k.wait(v_bn, L_WO)
                    k.wait(p_f[1], L_F)
                    v.tensor_tensor(fg[:, :], proj[:, 1, 0:FH], bp[:, bass.ds(at + FH, FH)], ALU.add).then_inc(v_fg, 1)
                if k.on(L_WO):
                    if not k.on(L_F):
                        k.wait(v_bn, L_WO)
                    v.bn_aggr(mv[:, :], st[:, :]).then_inc(v_mv, 1)
                if k.on(L_QKV):
                    k.wait(v_rs, L_QKV, per=RS_STEPS)
                    k.wait(g_tab, L_QKV, base=TILES - 1)
                    normalise(k, 0)
                if k.on(L_WO):
                    k.wait(v_mv, L_WO)
                    v.tensor_scalar(rt2[:, 0:1], mv[:, 1:2], 1e-5, None, ALU.add).then_inc(v_ve, 1)
                if k.on(L_F):
                    k.wait(a_gelu, L_F)
                    k.wait(p_hT, L_F + 1)
                    v.tensor_tensor(hh[:, 0:FH], fa[:, :], fg[:, :], ALU.mult).then_inc(v_fm, 1)
                if k.on(L_QKV):
                    cosine(k, 0)
                if k.on(L_WO):
                    k.wait(g_rstd, L_WO)
                    k.wait(p_xnT, L_WO + 1)
                    v.tensor_scalar(xn[:, :], xs2[:, :], mv[:, 0:1], rt2[:, 1:2], ALU.subtract,
                                    ALU.mult).then_inc(v_xn, 1)
                if k.on(L_S):
                    k.wait(p_S, L_S)
                    s4 = sps[:, :, :].rearrange("p t (a j) -> p t a j", j=2 * WIN)
                    v.tensor_reduce(mx[:, :], s4, AX, ALU.max).then_inc(v_mx, 1)
                if k.on(L_F2):
                    k.wait(v_z2a, L_F2)
                    k.wait(d_xs2, L_F2 - 1, per=64)
                    zs = Z[:, bass.ds(k.slot(L_F2), P)]
                    v.tensor_tensor(zs, zs, z2t[:, :], ALU.add).then_inc(v_z, 1)
                if k.on(L_S):
                    k.wait(v_mx, L_S)
                    k.wait(p_pT, L_S + 1)
                    v.tensor_tensor(prob[:, :, :, :].rearrange("p a t j -> p t a j"), s4,
                                    mx[:, :].rearrange("p (t a) -> p t a", t=2).unsqueeze(3)
                                    .to_broadcast([P, 2, PAIRS, 2 * WIN]), ALU.subtract).then_inc(v_sub, 1)
                if k.on(L_QKV):
                    normalise(k, 1)
                if k.on(L_QKV):
                    cosine(k, 1)

            v.memset(w2[:, :], 0.0).then_inc(c_zero, 1)
            dve.wait_ge(d_x, 16)
            for b in range(BATCH):
                norm_stats(1 + b, b)
            v.memset(kT[:, :, :], 0.0)
            v.memset(va[:, :, :], 0.0).then_inc(c_zero, 1)
            for b in range(BATCH):
                norm_apply(1 + b, b, zslot, v_z)

            def prepare():
                dve.wait_ge(d_mlp, 16 * len(mlp_consts))
                for n in range(DEPTH):
                    last = v.tensor_copy(oT[:, n, :], lnT[:, 1, n:n + 1].to_broadcast([P, P]))
                last.then_inc(c_lnb, 1)
                dve.wait_ge(d_late, 16 * len(late_consts))
                for n in range(DEPTH):
                    dve.wait_ge(c_bps, n + 1)
                    at = bp[:, 2 * n * FH:2 * (n + 1) * FH].rearrange("p (c n) -> p c n", c=2)
                    v.tensor_tensor(at, at, pairs[n % len(pairs)][:, :, 0:FH], ALU.add).then_inc(c_bp, 1)
                dve.wait_ge(c_bp, DEPTH)

            dve.wait_ge(c_zero, 2)
            dve.wait_ge(c_zero2, 1)
            pipeline(dve, 0, step, prepare)

            dve.wait_ge(d_x, 32)
            dve.wait_ge(v_z, TILES + N)
            for b in range(BATCH):
                s0 = (b * (POS + 1) + 1) * P
                part = qk[:, b * INNER:(b + 1) * INNER]
                v.scalar_tensor_tensor(out=part, in0=Z[:, s0:s0 + POS * P], scalar=0.5, in1=part,
                                       op0=ALU.mult, op1=ALU.add).then_inc(n_x1, 1)
                dve.wait_ge(n_x1, b + 1)
                norm_stats(3 + b, b)
            dve.wait_ge(p_kT, N)
            for b in range(BATCH):
                norm_apply(3 + b, b, lambda t: rot[:, t * P:(t + 1) * P], n_xn)
            for b in range(BATCH):
                dve.wait_ge(n_xn, b + 1)
                part = qk[:, b * INNER:(b + 1) * INNER]
                v.tensor_tensor(tiles3(part), tiles3(part), boB[:, :].unsqueeze(1).to_broadcast([P, POS, P]),
                                ALU.add).then_inc(r_bo, 1)
            dve.wait_ge(g_add[1], N)
            dve.wait_ge(p_wo, N)
            dve.wait_ge(c_sig, 1)
            for b in range(BATCH):
                dve.wait_ge(r_h, b + 1)
                if b:
                    dve.wait_ge(r_y, b)
                v.tensor_scalar(swp[:, :], proj[:, :, :].rearrange("p a b -> p (a b)"), cols[:, 0:1], cols[:, 2:3],
                                ALU.add, ALU.mult).then_inc(r_bh, 1)
                dve.wait_ge(r_bh, b + 1)
                ys = (oT[:, :, :].rearrange("p a b -> p (a b)"), rot[:, 0:INNER])[b]
                v.tensor_tensor_scan(ys, cols[:, 3:4].to_broadcast([P, SEQ]), swp[:, :], 0.0,
                                     ALU.mult, ALU.add).then_inc(r_y, 1)
            for b in range(BATCH):
                part = qk[:, b * INNER:(b + 1) * INNER]
                dve.wait_ge(r_o, b + 1)
                dve.wait_ge(r_bo, b + 1)
                v.tensor_tensor(part, part, (sps, ops)[b][:, :, :].rearrange("p a b -> p (a b)"),
                                ALU.add).then_inc(r_x2, 1)
                dve.wait_ge(r_x2, b + 1)
                norm_stats(5 + b, b)
            for b in range(BATCH):
                norm_apply(5 + b, b, zslot, v_z)
            pipeline(dve, 1, step)
            dve.wait_ge(d_x, 48)
            dve.wait_ge(v_z, 2 * (TILES + N))
            dve.wait_ge(p_kT, 2 * N)
            for b in range(BATCH):
                s0 = (b * (POS + 1) + 1) * P
                v.scalar_tensor_tensor(out=rot[:, b * INNER:(b + 1) * INNER], in0=Z[:, s0:s0 + POS * P],
                                       scalar=0.5, in1=qk[:, b * INNER:(b + 1) * INNER], op0=ALU.mult,
                                       op1=ALU.add).then_inc(f_out, 1)

        @block.gpsimd
        def _(pool):
            g_ = nc.gpsimd

            def tables(k, src, dst, scale):
                g_.tensor_tensor(tab[:, bass.ds(dst, 2 * DH)].rearrange("p (a d) -> p a d", d=DH),
                                 rope[:, bass.ds(src, 2 * DH)].rearrange("p (a d) -> p a d", d=DH),
                                 scl2[:, bass.ds(scale, DH)].unsqueeze(1).to_broadcast([P, 2, DH]),
                                 ALU.mult).then_inc(g_tab, 1)

            scl2 = scl[:, :, :, :].rearrange("p l k d -> p (l k d)")

            def step(k):
                if k.on(L_AV):
                    k.wait(v_rec, L_AV)
                    pr = prob[:, :, :, :].rearrange("p a t j -> p (a t) j")
                    g_.tensor_tensor(pr, pr, rr[:, :].unsqueeze(2).to_broadcast([P, HEADS, 2 * WIN]),
                                     ALU.mult).then_inc(g_nrm, 1)
                if k.on(L_WO):
                    k.wait(v_ve, L_WO)
                    k.wait(v_xn, L_WO + 1)
                    g_.tensor_tensor(rt2[:, 1:2], rt2[:, 0:1], half[:, 0:1], ALU.pow).then_inc(g_rstd, 1)
                if k.on(L_QKV):
                    po = k.off("pos", L_QKV, lambda u: (u % POS) * DH + ((u // TILES) % 2) * (4 * POS * DH))
                    hd = DH // 2
                    for g in range(2):
                        k.wait(v_t[g], L_QKV)
                        if g == 0:
                            k.wait(g_add[1], L_QKV + 1)
                        else:
                            k.wait(g_add[0], L_QKV)
                        src = qk[:, g * INNER:(g + 1) * INNER]
                        swapped = bass.AP(src.tensor, src.offset + hd,
                                          [list(src.ap[0]), [DH, HEADS], [-hd, 2], [1, hd]])
                        t = tab[:, bass.ds(po + (2 * g + 1) * POS * DH, DH)]
                        g_.tensor_tensor(halves(swp[:, :]), swapped,
                                         t.rearrange("p (a d) -> p a d", a=2).unsqueeze(1)
                                         .to_broadcast([P, HEADS, 2, hd]), ALU.mult).then_inc(g_B[g], 1)
                        k.wait(g_B[g], L_QKV)
                        k.wait(v_A[g], L_QKV)
                        r = rot[:, g * INNER:(g + 1) * INNER]
                        g_.tensor_tensor(r, r, swp[:, :], ALU.add).then_inc(g_add[g], 1)
                    src = k.off("rsrc", L_QKV, lambda u: (u % TILES) * (2 * DH))
                    dst = k.off("rdst", L_QKV, lambda u: ((u + TILES) % (2 * TILES)) * (2 * DH))
                    sc = k.off("rscl", L_QKV, lambda u: ((u - k.h * N) // 4) * DH + 4 * DH)
                    tables(k, src, dst, sc)

            def outer_pow(call, b):
                pool.wait_ge(n_eps, call)
                part = rstd[:, b * POS:(b + 1) * POS]
                g_.tensor_tensor(part, part, half[:, 0:POS], ALU.pow).then_inc(n_pow, 1)

            g_.memset(half[:, :], -0.5)
            g_.memset(kflag[:, :], 1.0).then_inc(c_kf, 1)
            pool.wait_ge(c_kf, 1)
            g_.memset(kflag[:, 0:1], 0.0)
            g_.memset(kflag[:, POS:POS + 1], 0.0)
            for ap in (Z[:, 0:P], Z[:, (POS + 1) * P:(POS + 2) * P], qTz[:, :, :, :, :], pTz[:, :, :, :, :], rt2[:, :]):
                g_.memset(ap, 0.0)
            g_.memset(hh[:, :], 0.0).then_inc(c_zero2, 1)
            pool.wait_ge(c_zero2, 1)
            for b in range(BATCH):
                outer_pow(1 + b, b)
            pool.wait_ge(d_const, 16 * len(consts))
            for kind in (0, 2):
                for a in range(2):
                    last = g_.tensor_copy(scl[:, 0:DEPTH, kind + 1, a * DH // 2:(a + 1) * DH // 2],
                                          scl[:, 0:DEPTH, kind, (1 - a) * DH // 2:(2 - a) * DH // 2])
            last.then_inc(c_scl, 1)
            pool.wait_ge(c_scl, 1)
            g_.tensor_copy(scl[:, DEPTH, :, :], scl[:, 0, :, :]).then_inc(c_scl, 1)
            pool.wait_ge(c_scl, 2)
            for t in range(TILES):
                tables(None, t * 2 * DH, t * 2 * DH, (t // 4) * DH)
            pipeline(pool, 0, step)
            for b in range(BATCH):
                outer_pow(3 + b, b)
            for b in range(BATCH):
                outer_pow(5 + b, b)
            pipeline(pool, 1, step)


_INS = ["L0_attn_x", "L0_attn_w_in", "L0_attn_b_in", "L0_attn_a", "L0_attn_b", "L0_attn_w_out", "L0_attn_b_out",
        "L0_ffn_Wqkv", "L0_ffn_q_scale", "L0_ffn_k_scale", "L0_ffn_Wo", "L0_ffn_ln_g", "L0_ffn_ln_b",
        "L0_ffn_W1", "L0_ffn_b1", "L0_ffn_W2", "L0_ffn_b2"]


def _constants():
    f = np.float32
    half = np.arange(0, DH, 2, dtype=f)
    inv_freq = (f(1.0) / np.power(f(10000.0), half / f(DH), dtype=f)).astype(f)
    t = np.arange(SEQ, dtype=f)
    freqs = t[:, None] * inv_freq[None, :]
    freqs = np.concatenate([freqs, freqs], -1)
    base = ((half + f(0.4 * DH)) / f(1.4 * DH)).astype(f)
    scale = np.power(base[None, :], ((t - SEQ // 2) / f(WIN // 2))[:, None], dtype=f)
    scale = np.concatenate([scale, scale], -1)
    sign = np.where(np.arange(DH) < DH // 2, f(-1), f(1))
    cos, sin = np.cos(freqs), np.sin(freqs) * sign
    kinds = np.stack([cos * scale * f(QK_SCALE), sin * scale * f(QK_SCALE), cos / scale, sin / scale])
    rope = kinds.reshape(4, POS, P, DH).transpose(2, 0, 1, 3).reshape(P, 4 * POS * DH).astype(f)
    row = np.arange(P)
    i, g = (row % WIN)[:, None], (row // (2 * WIN))[:, None]
    j = (np.arange(512) % (2 * WIN))[None, :]
    usual = ((j < WIN) & (j >= i)) | ((j >= WIN) & (j - WIN <= i))
    first = np.where(g == 0, usual & (j >= WIN), usual)
    mask = np.concatenate([np.where(m, 0.0, NEG) for m in (usual, first)], 1).astype(f)
    return {"rope": rope, "mask": mask, "ident": np.eye(P, dtype=f)}


def kernel(**inputs):
    import concourse.bacc as _bacc
    from concourse.bass_utils import run_bass_kernel_spmd as _run

    nc = _bacc.Bacc("TRN2", target_bir_lowering=False, num_devices=1)
    arrays, args = {}, []
    for name in _INS:
        a = np.ascontiguousarray(inputs[name])
        arrays[f"in_{name}"] = a
        args.append(nc.dram_tensor(f"in_{name}", a.shape, mybir.dt.from_np(a.dtype), kind="ExternalInput").ap())
    for name, a in _constants().items():
        arrays[f"const_{name}"] = a
        args.append(nc.dram_tensor(f"const_{name}", a.shape, mybir.dt.from_np(a.dtype), kind="ExternalInput").ap())
    x2 = nc.dram_tensor("x2_scratch", (P, TILES * P), F32).ap()
    out = nc.dram_tensor("out_0", (BATCH, SEQ, P), F32, kind="ExternalOutput").ap()
    macaron(nc, *args, x2, out)
    r = _run(nc, [arrays], core_ids=[0])
    return r.results[0]["out_0"]
```
